# Optimizing a Trainium2 kernel written in Bass

```python
import numpy as np
import jax
import jax.numpy as jnp

def _softmax(x, axis=-1):
    return jax.nn.softmax(x, axis=axis)

def _gelu(x):
    return jax.nn.gelu(x, approximate=True)

def _silu(x):
    return jax.nn.silu(x)

def _sigmoid(x):
    return jax.nn.sigmoid(x)

def _layernorm(x, axis=-1, eps=1e-05):
    m = jnp.mean(x, axis=axis, keepdims=True)
    v = jnp.var(x, axis=axis, keepdims=True)
    return (x - m) / jnp.sqrt(v + eps)

def _scatter_add(tgt, idx, src, axis=0):
    return tgt.at[idx].add(src)

def _segment_sum(src, seg, n):
    return jax.ops.segment_sum(src, seg, n)
kernel_name = 'mk_audio_tower_d2_tok_audfeat512_r4_caad82'

def setup_inputs(seed: int=0):
    np.random.seed(seed)
    _w = jnp.asarray

    def _rec_inputs():
        import jax
        import jax.numpy as jnp
        _rk = jax.random.key(seed)
        x = -0.000392918 + 0.999932 * jax.random.normal(jax.random.fold_in(_rk, 1), (8, 750, 128), jnp.float32)
        return x
    x = _rec_inputs()

    def _L0_tok_setup():
        import jax, jax.numpy as jnp
        import numpy as np
        K = 5
        DIL = 1
        C_IN = 128
        C_OUT = 128
        key = jax.random.key(seed)
        k1, k2, k3 = jax.random.split(key, 3)
        hidden_states = jax.random.normal(k1, (8, 1024, C_IN), dtype=jnp.float32)
        W = jax.random.normal(k2, (C_OUT, C_IN * K), dtype=jnp.float32) * 0.02
        b = jax.random.normal(k3, (C_OUT,), dtype=jnp.float32) * 0.02
        return {'hidden_states': hidden_states, 'W': W, 'b': b}
    _L0_tok_all = _L0_tok_setup()
    _L0_tok_in = {k: v for k, v in _L0_tok_all.items() if k in ('W', 'b')}
    del _L0_tok_all

    def _L0_attn_setup():
        import jax, jax.numpy as jnp
        import numpy as np
        import math
        D_MODEL = 128
        key = jax.random.key(seed)
        k1, k2, k3 = jax.random.split(key, 3)
        X = jax.random.normal(k1, (4, 2048, D_MODEL), dtype=jnp.float32)
        s = 1.0 / math.sqrt(D_MODEL)
        W_v = jax.random.uniform(k2, (D_MODEL, D_MODEL), dtype=jnp.float32, minval=-s, maxval=s)
        W_theta = jax.random.uniform(k3, (D_MODEL, D_MODEL), dtype=jnp.float32, minval=-s, maxval=s)
        return {'X': X, 'W_v': W_v, 'W_theta': W_theta}
    _L0_attn_all = _L0_attn_setup()
    _L0_attn_in = {k: v for k, v in _L0_attn_all.items() if k in ('W_v', 'W_theta')}
    del _L0_attn_all

    def _L0_ffn_setup():
        import jax, jax.numpy as jnp
        import numpy as np
        EPS = 1e-09
        LN_EPS = 1e-05

        def _layernorm(x, gamma):
            x = x.astype(jnp.float32)
            mu = jnp.mean(x, axis=-1, keepdims=True)
            var = jnp.var(x, axis=-1, keepdims=True)
            return (x - mu) * jax.lax.rsqrt(var + LN_EPS) * gamma
        key = jax.random.key(seed)
        ks = jax.random.split(key, 5)
        b, n, d, e, h = (4, 256, 128, 6, 512)
        x = jax.random.normal(ks[0], (b, n, d), dtype=jnp.float32)
        w_gating = jax.random.normal(ks[1], (d, e), dtype=jnp.float32)
        std1 = 1.0 / np.sqrt(h)
        std2 = 1.0 / np.sqrt(d)
        w1 = jax.random.uniform(ks[2], (e, d, h), jnp.float32, -std1, std1)
        w2 = jax.random.uniform(ks[3], (e, h, d), jnp.float32, -std2, std2)
        gamma = jnp.ones((d,), dtype=jnp.float32)
        return {'x': x, 'w_gating': w_gating, 'gamma': gamma, 'w1': w1, 'w2': w2}
    _L0_ffn_all = _L0_ffn_setup()
    _L0_ffn_in = {k: v for k, v in _L0_ffn_all.items() if k in ('w_gating', 'gamma', 'w1', 'w2')}
    del _L0_ffn_all

    def _L1_attn_setup():
        import jax, jax.numpy as jnp
        import numpy as np
        B, L, D, H = (4, 256, 128, 8)
        HD = D // H

        def _window_size(L):
            for cand in (5, 4, 3, 2):
                if L % cand == 0:
                    return cand
            return 5

        def _window_stats(attn, ws):
            b, h, l, _ = attn.shape
            nw = l // ws
            r = attn.reshape(b, h, nw, ws, l)
            mean = r.mean(axis=(-1, -2))
            std = jnp.std(r, axis=-1, ddof=1).mean(axis=-1)
            mx = r.max(axis=-1).mean(axis=-1)
            mn = r.min(axis=-1).mean(axis=-1)
            return jnp.stack([mean, std, mx, mn], axis=-1)
        key = jax.random.key(seed)
        ks = jax.random.split(key, 13)
        s = 0.02
        return {'x': jax.random.normal(ks[0], (B, L, D), jnp.float32), 'Wq1': jax.random.normal(ks[1], (D, D), jnp.float32) * s, 'Wk1': jax.random.normal(ks[2], (D, D), jnp.float32) * s, 'Wq2': jax.random.normal(ks[3], (D, D), jnp.float32) * s, 'Wk2': jax.random.normal(ks[4], (D, D), jnp.float32) * s, 'Wv': jax.random.normal(ks[5], (D, D), jnp.float32) * s, 'Wo': jax.random.normal(ks[6], (D, D), jnp.float32) * s, 'gw1': jax.random.normal(ks[7], (8, 32), jnp.float32) * 0.1, 'gb1': jnp.zeros((32,), jnp.float32), 'gw2': jax.random.normal(ks[8], (32, 16), jnp.float32) * 0.1, 'gb2': jnp.zeros((16,), jnp.float32), 'gw3': jax.random.normal(ks[9], (16, 1), jnp.float32) * 0.1, 'gb3': jnp.zeros((1,), jnp.float32)}
    _L1_attn_all = _L1_attn_setup()
    _L1_attn_in = {k: v for k, v in _L1_attn_all.items() if k in ('Wq1', 'Wk1', 'Wq2', 'Wk2', 'Wv', 'Wo', 'gw1', 'gb1', 'gw2', 'gb2', 'gw3', 'gb3')}
    del _L1_attn_all

    def _L1_ffn_setup():
        import jax, jax.numpy as jnp
        import numpy as np
        CAPACITY_FACTOR = 1.2
        key = jax.random.key(seed)
        k1, k2, k3 = jax.random.split(key, 3)
        B, S, D, E = (8, 1024, 128, 16)
        x = jax.random.normal(k1, (B, S, D), dtype=jnp.float32)
        switch_w = jax.random.normal(k2, (E, D), dtype=jnp.float32) * 0.02
        switch_b = jnp.zeros((E,), dtype=jnp.float32)
        expert_w = jax.random.normal(k3, (E, D, D), dtype=jnp.float32) * 0.02
        expert_b = jnp.zeros((E, D), dtype=jnp.float32)
        return {'x': x, 'switch_w': switch_w, 'switch_b': switch_b, 'expert_w': expert_w, 'expert_b': expert_b}
    _L1_ffn_all = _L1_ffn_setup()
    _L1_ffn_in = {k: v for k, v in _L1_ffn_all.items() if k in ('switch_w', 'switch_b', 'expert_w', 'expert_b')}
    del _L1_ffn_all
    return {'x': x, 'L0_tok_W': _L0_tok_in['W'], 'L0_tok_b': _L0_tok_in['b'], 'L0_attn_W_v': _L0_attn_in['W_v'], 'L0_attn_W_theta': _L0_attn_in['W_theta'], 'L0_ffn_w_gating': _L0_ffn_in['w_gating'], 'L0_ffn_gamma': _L0_ffn_in['gamma'], 'L0_ffn_w1': _L0_ffn_in['w1'], 'L0_ffn_w2': _L0_ffn_in['w2'], 'L1_attn_Wq1': _L1_attn_in['Wq1'], 'L1_attn_Wk1': _L1_attn_in['Wk1'], 'L1_attn_Wq2': _L1_attn_in['Wq2'], 'L1_attn_Wk2': _L1_attn_in['Wk2'], 'L1_attn_Wv': _L1_attn_in['Wv'], 'L1_attn_Wo': _L1_attn_in['Wo'], 'L1_attn_gw1': _L1_attn_in['gw1'], 'L1_attn_gb1': _L1_attn_in['gb1'], 'L1_attn_gw2': _L1_attn_in['gw2'], 'L1_attn_gb2': _L1_attn_in['gb2'], 'L1_attn_gw3': _L1_attn_in['gw3'], 'L1_attn_gb3': _L1_attn_in['gb3'], 'L1_ffn_switch_w': _L1_ffn_in['switch_w'], 'L1_ffn_switch_b': _L1_ffn_in['switch_b'], 'L1_ffn_expert_w': _L1_ffn_in['expert_w'], 'L1_ffn_expert_b': _L1_ffn_in['expert_b']}

def reference(x, L0_tok_W, L0_tok_b, L0_attn_W_v, L0_attn_W_theta, L0_ffn_w_gating, L0_ffn_gamma, L0_ffn_w1, L0_ffn_w2, L1_attn_Wq1, L1_attn_Wk1, L1_attn_Wq2, L1_attn_Wk2, L1_attn_Wv, L1_attn_Wo, L1_attn_gw1, L1_attn_gb1, L1_attn_gw2, L1_attn_gb2, L1_attn_gw3, L1_attn_gb3, L1_ffn_switch_w, L1_ffn_switch_b, L1_ffn_expert_w, L1_ffn_expert_b):
    import jax
    import jax.numpy as jnp

    def _L0_tok_ref(hidden_states, W, b):
        import jax, jax.numpy as jnp
        import numpy as np
        K = 5
        DIL = 1
        C_IN = 128
        C_OUT = 128
        B, T, C = hidden_states.shape
        L = T - DIL * (K - 1)
        patches = jnp.stack([hidden_states[:, i * DIL:i * DIL + L, :] for i in range(K)], axis=2)
        patches = patches.reshape(B, L, K * C)
        out = jnp.einsum('blf,of->blo', patches, W) + b
        return jax.nn.relu(out)

    def _L0_attn_ref(X, W_v, W_theta):
        import jax, jax.numpy as jnp
        import numpy as np
        import math
        D_MODEL = 128
        n = X.shape[1]
        d = X.shape[2]
        XW_v = X @ W_v.T
        theta_X = X @ W_theta.T
        first_term = jnp.mean(XW_v, axis=1, keepdims=True)
        kv = jnp.einsum('bnd,bne->bde', theta_X, XW_v)
        second_term = X @ kv / (n * math.sqrt(d))
        return first_term + second_term

    def _L0_ffn_ref(x, w_gating, gamma, w1, w2):
        import jax, jax.numpy as jnp
        import numpy as np
        EPS = 1e-09
        LN_EPS = 1e-05

        def _layernorm(x, gamma):
            x = x.astype(jnp.float32)
            mu = jnp.mean(x, axis=-1, keepdims=True)
            var = jnp.var(x, axis=-1, keepdims=True)
            return (x - mu) * jax.lax.rsqrt(var + LN_EPS) * gamma
        b, n, d = x.shape
        E = w_gating.shape[-1]
        C = max(min(n, int(n * 6.0 / E)), 4)
        raw = jnp.einsum('bnd,de->bne', x, w_gating)
        probs = jax.nn.softmax(raw, axis=-1)
        gate1 = jnp.max(probs, axis=-1)
        idx1 = jnp.argmax(probs, axis=-1)
        mask1 = jax.nn.one_hot(idx1, E, dtype=jnp.float32)
        gates_wo1 = probs * (1.0 - mask1)
        gate2 = jnp.max(gates_wo1, axis=-1)
        denom = gate1 + gate2 + EPS
        gate1 = gate1 / denom
        pos1 = (jnp.cumsum(mask1, axis=-2) - mask1) * mask1
        mask1 = mask1 * (pos1 < float(C)).astype(jnp.float32)
        mask1_flat = jnp.sum(mask1, axis=-1)
        pos1_flat = jnp.sum(pos1, axis=-1).astype(jnp.int32)
        gate1 = gate1 * mask1_flat
        combine = gate1[..., None, None] * mask1_flat[..., None, None] * jax.nn.one_hot(idx1, E, dtype=jnp.float32)[..., None] * jax.nn.one_hot(pos1_flat, C, dtype=jnp.float32)[..., None, :]
        dispatch = (combine != 0).astype(jnp.float32)
        expert_in = jnp.einsum('bnd,bnec->ebcd', x, dispatch)
        xn = _layernorm(expert_in, gamma)
        hidden = jax.nn.gelu(jnp.einsum('ebcd,edh->ebch', xn, w1), approximate=False)
        expert_out = jnp.einsum('ebch,ehd->ebcd', hidden, w2)
        out = jnp.einsum('ebcd,bnec->bnd', expert_out, combine)
        return out

    def _L1_attn_ref(x, Wq1, Wk1, Wq2, Wk2, Wv, Wo, gw1, gb1, gw2, gb2, gw3, gb3):
        import jax, jax.numpy as jnp
        import numpy as np
        B, L, D, H = (4, 256, 128, 8)
        HD = D // H

        def _window_size(L):
            for cand in (5, 4, 3, 2):
                if L % cand == 0:
                    return cand
            return 5

        def _window_stats(attn, ws):
            b, h, l, _ = attn.shape
            nw = l // ws
            r = attn.reshape(b, h, nw, ws, l)
            mean = r.mean(axis=(-1, -2))
            std = jnp.std(r, axis=-1, ddof=1).mean(axis=-1)
            mx = r.max(axis=-1).mean(axis=-1)
            mn = r.min(axis=-1).mean(axis=-1)
            return jnp.stack([mean, std, mx, mn], axis=-1)
        b, l, d = x.shape
        hd = d // H
        scale = 1.0 / jnp.sqrt(jnp.float32(hd))

        def heads(y):
            return y.reshape(b, l, H, hd).transpose(0, 2, 1, 3)
        q1, k1 = (heads(x @ Wq1), heads(x @ Wk1))
        q2, k2 = (heads(x @ Wq2), heads(x @ Wk2))
        v = heads(x @ Wv)
        attn1 = jax.nn.softmax(jnp.einsum('bhqd,bhkd->bhqk', q1, k1) * scale, axis=-1)
        attn2 = jax.nn.softmax(jnp.einsum('bhqd,bhkd->bhqk', q2, k2) * scale, axis=-1)
        ws = _window_size(l)
        gate_in = jnp.concatenate([_window_stats(attn1, ws), _window_stats(attn2, ws)], axis=-1)
        hid = jax.nn.relu(gate_in @ gw1 + gb1)
        hid = jax.nn.relu(hid @ gw2 + gb2)
        alpha = jax.nn.sigmoid(hid @ gw3 + gb3)
        alpha_full = jnp.repeat(alpha, ws, axis=2)
        fused = alpha_full * attn1 + (1.0 - alpha_full) * attn2
        out = jnp.einsum('bhqk,bhkd->bhqd', fused, v)
        out = out.transpose(0, 2, 1, 3).reshape(b, l, d)
        return out @ Wo

    def _L1_ffn_ref(x, switch_w, switch_b, expert_w, expert_b):
        import jax, jax.numpy as jnp
        import numpy as np
        CAPACITY_FACTOR = 1.2
        B, S, D = x.shape
        E = switch_w.shape[0]
        N = B * S
        xf = x.reshape(N, D)
        logits = xf @ switch_w.T + switch_b
        probs = jax.nn.softmax(logits, axis=-1)
        route_probs = jnp.max(probs, axis=-1)
        routes = jnp.argmax(probs, axis=-1)
        oh = jax.nn.one_hot(routes, E, dtype=jnp.int32)
        pos = jnp.take_along_axis(jnp.cumsum(oh, axis=0), routes[:, None], axis=1)[:, 0] - 1
        capacity = int(CAPACITY_FACTOR * N / E)
        keep = pos < capacity
        buf = jnp.zeros((E, capacity, D), dtype=xf.dtype).at[routes, pos].set(xf)
        y = jnp.einsum('ecd,efd->ecf', buf, expert_w) + expert_b[:, None, :]
        gathered = y[routes, jnp.minimum(pos, capacity - 1)]
        out = jnp.where(keep[:, None], gathered, xf) * route_probs[:, None]
        return out.reshape(B, S, D)
    h = _L0_tok_ref(x, L0_tok_W, L0_tok_b)
    h = h + _L0_attn_ref(_layernorm(h, axis=-1), L0_attn_W_v, L0_attn_W_theta)
    h = h + _L0_ffn_ref(_layernorm(h, axis=-1), L0_ffn_w_gating, L0_ffn_gamma, L0_ffn_w1, L0_ffn_w2)
    h = h + _L1_attn_ref(_layernorm(h, axis=-1), L1_attn_Wq1, L1_attn_Wk1, L1_attn_Wq2, L1_attn_Wk2, L1_attn_Wv, L1_attn_Wo, L1_attn_gw1, L1_attn_gb1, L1_attn_gw2, L1_attn_gb2, L1_attn_gw3, L1_attn_gb3)
    h = h + _L1_ffn_ref(_layernorm(h, axis=-1), L1_ffn_switch_w, L1_ffn_switch_b, L1_ffn_expert_w, L1_ffn_expert_b)
    return h

_drawn_inputs = setup_inputs


def setup_inputs(seed=0):
    import zlib

    import numpy as np

    out = dict(_drawn_inputs(seed))
    spreads = {'L0_ffn_gamma': (1.0, 0.2),
     'L1_attn_gb1': (0.0, 0.8),
     'L1_attn_gb2': (0.0, 0.8),
     'L1_ffn_switch_b': (0.0, 0.1),
     'L1_ffn_expert_b': (0.0, 0.428)}
    factors = {'L1_attn_Wq1': 8.0,
     'L1_attn_Wk1': 8.0,
     'L1_attn_Wq2': 8.0,
     'L1_attn_Wk2': 8.0,
     'L1_attn_Wv': 2.693,
     'L1_attn_gw1': 8.0,
     'L1_attn_gw2': 8.0,
     'L1_attn_gw3': 8.0}
    for name, (base, spread) in spreads.items():
        noise = np.random.default_rng([zlib.crc32(name.encode()), seed]).standard_normal(out[name].shape)
        drawn = base * np.exp(spread * noise) if base else spread * noise
        out[name] = jnp.asarray(drawn.astype(out[name].dtype))
    for name, factor in factors.items():
        out[name] = (out[name] * factor).astype(out[name].dtype)
    return out
```

```python
from contextlib import ExitStack

import concourse.bass as bass
from concourse import mybir

F32 = mybir.dt.float32
BF16 = mybir.dt.bfloat16
ALU = mybir.AluOpType
ACT = mybir.ActivationFunctionType
X_AXIS = mybir.AxisListType.X
XY_AXES = mybir.AxisListType.XY

P = 128
B = 8
T_IN = 750
C = 128
TAPS = 5
L = T_IN - (TAPS - 1)
R = 2
W = L // R
WT = 3
NT = R * WT
PITCH = WT * P
N_LAST = W - (WT - 1) * P
ROWS = [P, P, N_LAST] * R
N_ALL = R * PITCH
W_IN = T_IN // R

E0 = 6
HID = 512
HC = HID // P
H = 8
HD = C // H
VD = HD + 1
PARTS = 3
TERMS = 6
SK = TERMS * HD
SHIFT0 = SK
STACK = SK + PARTS
SLOTS = 4
STEPS = B * H * 2
BODIES = STEPS // SLOTS
ERING = 4
LAG = 2
PE_LAG = LAG * NT + 1
OT_ROWS = 3 * 32 + VD
E1 = 16
CAPACITY = int(1.2 * B * L / E1)
LN_EPS = 1e-5
GATE_EPS = 1e-9
GH1 = 32
GH2 = 16
NST = 3

NLN0 = 4


def tile_cols(t):
    return (t // WT) * PITCH + (t % WT) * P


def need(eng, sem, value):
    if isinstance(value, int) and value <= 0:
        return
    eng.wait_ge(sem, value)


def settle(eng, passed):
    eng.sem_inc(passed, 1)


class Chain:

    def __init__(self, eng, sem, base):
        self.eng, self.sem, self.base, self.n = eng, sem, base, 0

    def mark(self, ins):
        ins.then_inc(self.sem, 1)
        self.n += 1

    def sync(self):
        self.eng.wait_ge(self.sem, self.base + self.n)

    def link(self, ins):
        self.mark(ins)
        self.sync()


def norm_base(i):
    if isinstance(i, int):
        return 3 * min(i, B) + max(0, i - 2)
    return i * NLN0 - 2


def n_slot(slot, kt):
    return (NT * slot + kt) % ERING


def earlier(g, slot, lag):
    return (g, slot - lag) if slot >= lag else (g - 1, slot - lag + SLOTS)


def ffn_slots():
    out = []
    for e in range(E0):
        out += [("up", e, 0), ("up", e, 1)]
        if e:
            out.append(("down", e - 1))
        out += [("up", e, 2), ("up", e, 3)]
    return out + [("down", E0 - 1)]


FRONT = ["xt", "conv", "gram", "gram_v", "kv", "x1t", "attn", "xrt", "route"]
BACK = ["x3t", "qk0", "qk1", "qk2", "qk3", "v"]


def plan(front, ffn, back):
    small = [("back", x) for x in BACK] * back + [("front", x) for x in FRONT] * front
    big = [("ffn", x) for x in ffn_slots()] * ffn
    out = []
    every = max(1, len(big) // (len(small) + 1)) if small else 1
    while big or small:
        out += big[:every]
        big = big[every:]
        if small:
            out.append(small.pop(0))
    if ffn:
        out.append(("ffn", ("end",)))
    if front:
        out.append(("front", "handover"))
    return out


def build(nc, x, L0_tok_W, L0_tok_b, L0_attn_W_v, L0_attn_W_theta, L0_ffn_w_gating, L0_ffn_gamma,
          L0_ffn_w1, L0_ffn_w2, L1_attn_Wq1, L1_attn_Wk1, L1_attn_Wq2, L1_attn_Wk2, L1_attn_Wv,
          L1_attn_Wo, L1_attn_gw1, L1_attn_gb1, L1_attn_gw2, L1_attn_gb2, L1_attn_gw3,
          L1_attn_gb3, L1_ffn_switch_w, L1_ffn_switch_b, L1_ffn_expert_w, L1_ffn_expert_b, out):
    ctx = ExitStack()
    with ctx:
        def sb(name, shape, dt=F32):
            return ctx.enter_context(nc.sbuf_tensor(name, shape, dt))

        def sem(name):
            return ctx.enter_context(nc.semaphore(name))

        parts_dram = nc.dram_tensor("parts_dram", (B * H, 4, PARTS, HD, N_ALL), BF16).ap()

        max_dram = nc.dram_tensor("max_dram", (SLOTS, PARTS, NT, P), BF16).ap()

        ident = sb("ident", [P, P])
        before = sb("before", [P, P], BF16)
        ones_bf = sb("ones_bf", [P, P], BF16)
        minus_half = sb("minus_half", [P, 1])
        plus_half = sb("plus_half", [P, 1])
        pick = sb("pick", [P, R * VD])
        rank_desc = sb("rank_desc", [P, E1])
        arena = sb("arena", [P, STEPS * NT * (VD + NST)])
        hid = [arena[:, i * HC * N_ALL:(i + 1) * HC * N_ALL].rearrange("p (k n) -> p k n", k=HC) for i in range(2)]
        w1_at = 2 * HC * N_ALL
        w1 = arena[:, w1_at:w1_at + E0 * HID].rearrange("p (e h) -> p e h", e=E0)
        w2_at = w1_at + E0 * HID
        w2 = arena[:, w2_at:w2_at + E0 * HC * C].rearrange("p (e k d) -> p e k d", e=E0, k=HC)
        nat_at = w2_at + E0 * HC * C
        w_nat = arena[:, nat_at:nat_at + (TAPS + 2 + E1) * P].rearrange("p (n c) -> p n c", c=P)
        o_all = arena[:, 0:STEPS * NT * VD].rearrange("p (j v) -> p j v", j=STEPS)
        stat_all = arena[:, STEPS * NT * VD:].rearrange("p (j v) -> p j v", j=STEPS)
        w_t = sb("w_t", [P, TAPS + 2 + E1, P])
        sw_nat = sb("sw_nat", [E1, P])
        sw_t = sb("sw_t", [P, E1])
        conv_b = sb("conv_b", [P, C])
        w_gate = sb("w_gate", [P, E0])
        gamma = sb("gamma", [P, 1])
        w_qk = sb("w_qk", [P, 4, C])
        w_v = sb("w_v", [P, C])
        w_o = sb("w_o", [P, C])
        g1 = sb("g1", [H * 8, H * GH1])
        g2 = sb("g2", [P, H * GH2 // 2])
        g3 = sb("g3", [P, H])
        gb1 = sb("gb1", [P, 1])
        gb2 = sb("gb2", [P, 1])
        gb3 = sb("gb3", [P, 1])
        ngb3 = sb("ngb3", [P, 1])
        sw_b = sb("sw_b", [P, E1])
        ex_b = sb("ex_b", [E1, C])

        def conv_w(i):
            return w_t[:, i, :]

        wv0_t = w_t[:, TAPS, :]
        wth_t = w_t[:, TAPS + 1, :]

        xin = sb("xin", [P, WT, R * C])
        x_t = sb("x_t", [P, R, PITCH + 2])
        h_cur = sb("h_cur", [P, NT, C])
        bn = sb("bn", [P, NT, 6])
        mv = sb("mv", [P, NT, 2])
        var_eps = sb("var_eps", [P, NT])
        rstd = sb("rstd", [P, NT])
        x1 = sb("x1", [P, NT, C + 1])
        x1_t = sb("x1_t", [P, N_ALL])
        gram = sb("gram", [P, C])
        x_mean = sb("x_mean", [P, P])
        gram_v = sb("gram_v", [P, C])
        kv = sb("kv", [P, C])
        xr = sb("xr", [P, NT, C])
        xr_t = sb("xr_t", [P, N_ALL])
        xf = sb("xf", [P, NT, C])
        xf_t = sb("xf_t", [P, N_ALL])
        r_a = sb("r_a", [P, NT, E1])
        r_b = sb("r_b", [P, NT, E1])
        r_c = sb("r_c", [P, NT, E1])
        r_p = sb("r_p", [P, NT, E1])
        r_m = sb("r_m", [P, NT])
        r_n = sb("r_n", [P, NT])
        r_g = sb("r_g", [P, NT])
        comb_next = sb("comb_next", [P, NT, E0])
        comb = sb("comb", [P, NT, E0])
        h_acc = sb("h_acc", [P, NT, C])
        h_two = sb("h_two", [P, NT, C])
        x3 = sb("x3", [P, NT, C])
        x3_t = sb("x3_t", [P, N_ALL])
        parts = sb("parts", [P, 4, PARTS, N_ALL], BF16)
        rest = sb("rest", [P, N_ALL])
        h_all = sb("h_all", [P, B, NT * C])
        v_all = sb("v_all", [P, B, NT * H, VD])

        ps = ctx.enter_context(nc.psum_tensor("ps", [P, 8, 512], F32))

        def pair(k):
            return ps[:, 2 * k:2 * k + 2, 0:PITCH]

        def pair_tile(k, t):
            return ps[:, 2 * k + t // WT, (t % WT) * P:(t % WT + 1) * P]

        def as_pair(ap):
            if len(ap.shape) == 3:
                return ap.rearrange("p (r w) c -> p r (w c)", r=R)
            return ap.rearrange("p (r c) -> p r c", r=R)

        s = {}
        for name in ("w_loaded", "w_ready", "const_ready", "dve_passed", "act_passed", "pool_passed", "pe_passed", "nat_ps", "nat_sb", "x_loaded", "dve_step",
                     "act_step", "pool_step", "var_ready", "rstd_ready",
                     "xt_ps", "xt_sb", "conv_ps", "x1_sb", "gram_ps", "gram_sb", "gram_v_ps", "gram_v_sb",
                     "kv_ps", "kv_sb", "x1t_ps", "x1t_sb", "attn_ps", "xr_sb", "xrt_ps", "xrt_sb",
                     "route_ps", "logit_sb", "exp_sb", "xf_sb", "xft_ps", "xft_sb", "comb_sb", "up_ps", "hid_sb",
                     "down_ps", "ffn_acc", "h2_sb", "h_stored", "x3_sb", "x3t_ps", "x3t_sb", "qk_ps",
                     "part1_sb", "qk_split", "v_ps", "v_sb", "p1_done",
                     "row_scored", "neg_max", "row_exp", "min_done", "max_parts", "max_turned", "max_stored",
                     "t_scored", "t_exp", "av_done", "ot_sb", "o_turned", "o_copied", "vh_ready", "stat_saved",
                     "go2", "feat_ready", "pow_in", "pow_out", "feat_ps", "feat_sb", "g1_ps", "g1_sb", "g2_ps",
                     "g2_sb", "g3_ps", "g3_sb", "fused", "fused_ps", "fused_sb", "wo_ps", "x4_sb", "x4t_ps",
                     "x4t_sb", "route1_ps", "logit1_sb", "exp1_sb", "onehot", "rank_ps", "mask_sb", "mask_ps", "maskt_sb",
                     "bias_ps", "bias_used", "ex_ps", "ex_used", "y_ready", "y_stored"):
            s[name] = sem(name)
        parts_stored = [sem(f"parts_stored{i}") for i in range(4)]
        stack_loaded = [sem(f"stack_loaded{i}") for i in range(SLOTS)]
        shift_loaded = [sem(f"shift_loaded{i}") for i in range(SLOTS)]

        weight_loads = [
            (w_nat[:, 0:TAPS, :], L0_tok_W.rearrange("o (i c) -> o i c", i=TAPS)),
            (w_nat[:, TAPS, :], L0_attn_W_v),
            (w_nat[:, TAPS + 1, :], L0_attn_W_theta),
            (w_nat[:, TAPS + 2:, :], L1_ffn_expert_w.rearrange("e f d -> f e d")),
            (sw_nat[:, :], L1_ffn_switch_w),
            (conv_b[:, :], L0_tok_b.partition_broadcast(P)),
            (w_gate[:, :], L0_ffn_w_gating),
            (gamma[:, :], L0_ffn_gamma.rearrange("(d o) -> d o", o=1)),
            (w1[:, :, :], L0_ffn_w1.rearrange("e d h -> d e h")),
            (w_qk[:, 0, :], L1_attn_Wq1), (w_qk[:, 1, :], L1_attn_Wk1),
            (w_qk[:, 2, :], L1_attn_Wq2), (w_qk[:, 3, :], L1_attn_Wk2),
            (w_v[:, :], L1_attn_Wv), (w_o[:, :], L1_attn_Wo),
            (sw_b[:, :], L1_ffn_switch_b.partition_broadcast(P)),
            (ex_b[:, :], L1_ffn_expert_b),
            (gb3[:, :], L1_attn_gb3.partition_broadcast(P)),
        ]
        for e in range(E0):
            weight_loads.append((w2[:, e, :, :], L0_ffn_w2[e].rearrange("(k h) d -> h k d", k=HC)))
        for i in range(H):
            weight_loads.append((g1[8 * i:8 * i + 8, GH1 * i:GH1 * (i + 1)], L1_attn_gw1))
            weight_loads.append((g3[GH2 * i:GH2 * (i + 1), i:i + 1], L1_attn_gw3))
            weight_loads.append((gb2[GH2 * i:GH2 * (i + 1), :], L1_attn_gb2.rearrange("(d o) -> d o", o=1)))
        for i in range(H // 2):
            weight_loads.append((g2[GH1 * i:GH1 * (i + 1), GH2 * i:GH2 * (i + 1)], L1_attn_gw2))
            weight_loads.append((gb1[GH1 * i:GH1 * (i + 1), :], L1_attn_gb1.rearrange("(d o) -> d o", o=1)))
        N_WLOAD = 16 * len(weight_loads)

        stacks = parts[0:STACK, :, :, :].rearrange("p n a c -> p (n a) c")
        q_st = [stacks[:, i, :] for i in range(SLOTS)]
        k_st = [stacks[:, SLOTS + i, :] for i in range(SLOTS)]
        stat = [sb(f"stat{i}", [P, NST, NT]) for i in range(SLOTS)]
        mp = [sb(f"mp{i}", [P, 32], BF16) for i in range(2)]
        mp_r = sb("mp_r", [P, 2, NT])
        mp_t = [sb(f"mp_t{i}", [P, 32], BF16) for i in range(SLOTS)]
        f_ring = [a[:, 0:R * W].rearrange("p (r w) -> p r w", r=R) for a in (
            xin[:, :, :].rearrange("p a c -> p (a c)"), rest, x_t[:, :, :].rearrange("p r w -> p (r w)"),
            x1[:, :, :].rearrange("p t c -> p (t c)"))]
        e_ring = [as_pair(a[:, :]) for a in (x1_t, xr_t, xf_t, x3_t)]
        o_t = [h_cur[:, :, :].rearrange("p t c -> p (t c)")[:, i * PITCH:i * PITCH + W] for i in range(2)]
        v_head = [sb(f"v_head{i}", [P, NT, VD]) for i in range(2)]

        h3, y, x4, x4_t, fo_t = h_cur, h_acc, xr, xr_t, xf_t
        inv_s = sb("inv_s", [P, H * 2, NT])
        sum_p = sb("sum_p", [P, H * 2, NT])
        sq_p = sb("sq_p", [P, H * 2, NT])
        pw_in = sb("pw_in", [P, 2, H * 2 * NT])
        pw_out = sb("pw_out", [P, 2, H * 2 * NT])
        feat = sb("feat", [P, WT, H, 2, 4])
        feat_t = sb("feat_t", [H * 8, PITCH])
        hid1 = x1_t[:, :].rearrange("p (a w) -> p a w", a=2)
        hid2 = sb("hid2", [P, PITCH])
        alpha = sb("alpha", [P, WT, H])
        beta = sb("beta", [P, WT, H])
        coef = sb("coef", [P, 2, H, NT])
        fo = [a[:, :, :].rearrange("p t (h d) -> p t h d", h=H) for a in (xf, x3)]
        oh = sb("oh", [P, NT, E1])
        ohs = sb("ohs", [P, WT, E1], BF16)
        carry = sb("carry", [P, E1])
        mask = sb("mask", [P, NT, E1])
        mask_t = sb("mask_t", [E1, N_ALL])
        self_c = sb("self_c", [P, NT])

        N_NAT = TAPS + 2 + E1
        x_view = x.rearrange("b (w r) c -> b w (r c)", r=R)
        out_view = out.rearrange("b (w r) c -> b w r c", r=R)

        block = ctx.enter_context(nc.Block())

        def first_part(run):
            run(0, plan(True, False, False))
            run(1, plan(True, True, False))
            return plan(True, True, True)

        @block.sync
        def _(sp):
            for dst, src in weight_loads[:9]:
                sp.dma_start(dst, src).then_inc(s["w_loaded"], 16)

            def load_x(b):
                need(sp, s["xt_ps"], b)
                sp.dma_start(xin[:, 0:2, :], x_view[b, 0:2 * P, :].rearrange("(a p) c -> p a c", p=P)).then_inc(s["x_loaded"], 16)
                sp.dma_start(xin[0:W_IN - 2 * P, 2, :], x_view[b, 2 * P:W_IN, :]).then_inc(s["x_loaded"], 16)

            def store_parts(b):
                for n in range(4):
                    need(sp, s["qk_split"], 4 * b + n + 1)
                    for h in range(H):
                        sp.dma_start(parts_dram[b * H + h, n].rearrange("a d c -> d a c"),
                                     parts[h * HD:(h + 1) * HD, n, :, :]).then_inc(parts_stored[n], 16)

            need(sp, s["const_ready"], 1)
            load_x(0)
            for dst, src in weight_loads[9:]:
                sp.dma_start(dst, src).then_inc(s["w_loaded"], 16)
            load_x(1)
            with sp.Fori(2, B) as i:
                store_parts(i - 2)
                load_x(i)
            store_parts(B - 2)
            store_parts(B - 1)
            for n in range(4):
                sp.wait_ge(parts_stored[n], 16 * H * B)

            def load_stacks(bh, m, slot, j):
                need(sp, s["t_scored"], NT * (j - SLOTS + 1))
                q, k = parts_dram[bh, 2 * m], parts_dram[bh, 2 * m + 1]
                row = 0
                for p in range(PARTS):
                    n = (PARTS - p) * HD
                    sp.dma_start(q_st[slot][row:row + n, :],
                                 q[0:PARTS - p].rearrange("a d c -> (a d) c")).then_inc(stack_loaded[slot], 16)
                    for a in range(PARTS - p):
                        sp.dma_start(k_st[slot][row + a * HD:row + (a + 1) * HD, :],
                                     k[p]).then_inc(stack_loaded[slot], 16)
                    row += n

            def load_shift(slot, j):
                need(sp, s["max_turned"], j + 1)
                for q in range(4):
                    sp.dma_start(max_dram[slot].rearrange("a t w -> (a t) w")[:, 32 * q:32 * q + 32],
                                 mp_t[slot][32 * q:32 * q + PARTS * NT, :]).then_inc(s["max_stored"], 16)
                sp.wait_ge(s["max_stored"], 64 * (j + 1))
                sp.dma_start(q_st[slot][SHIFT0:STACK, :],
                             max_dram[slot].rearrange("a t w -> a (t w)")).then_inc(shift_loaded[slot], 16)

            def steps(g, last):
                for slot in range(SLOTS):
                    j = g * SLOTS + slot
                    load_shift(slot, j)
                    nxt = slot + SLOTS - 1
                    if nxt >= SLOTS and last:
                        continue
                    load_stacks(g * 2 + nxt // 2, nxt % 2, nxt % SLOTS, j + SLOTS - 1)

            for j in range(SLOTS - 1):
                load_stacks(j // 2, j % 2, j, j)
            steps(0, False)
            with sp.Fori(1, BODIES - 1) as g:
                steps(g, False)
            steps(BODIES - 1, True)

            def store_y(b):
                sp.wait_ge(s["y_ready"], b + 1)
                for wt in range(WT):
                    n = ROWS[wt]
                    sp.dma_start(out_view[b, wt * P:wt * P + n, :, :],
                                 y[0:n, wt:NT:WT, :]).then_inc(s["y_stored"], 16)

            with sp.Fori(0, B) as b:
                store_y(b)
            sp.wait_ge(s["y_stored"], 16 * WT * B)

        @block.tensor
        def _(pe):
            def turn(k, src):
                for t in range(NT):
                    last = nc.tensor.transpose(pair_tile(k, t), src[:, t, 0:C], ident[:, :])
                return last

            def per_tile(k, stationary, moving):
                for t in range(NT):
                    for n, (lhs, rhs) in enumerate(zip(stationary, moving)):
                        last = nc.tensor.matmul(pair_tile(k, t), lhs(t), rhs, start=(n == 0), stop=(n == len(moving) - 1))
                return last

            pe.wait_ge(s["w_loaded"], N_WLOAD)
            pe.wait_ge(s["const_ready"], 2)
            for n in range(N_NAT + 1):
                if n >= 8:
                    pe.wait_ge(s["nat_sb"], n - 7)
                if n < N_NAT:
                    nc.tensor.transpose(ps[:, n % 8, 0:P], w_nat[:, n, :], ident[:, :]).then_inc(s["nat_ps"], 1)
                else:
                    nc.tensor.transpose(ps[:, n % 8, 0:E1], sw_nat[:, :], ident[0:E1, 0:E1]).then_inc(s["nat_ps"], 1)
            pe.wait_ge(s["nat_sb"], N_NAT + 1)

            def cols(buf):
                return lambda t: buf[:, tile_cols(t):tile_cols(t) + P]

            def front(item, b):
                if item == "xt":
                    need(pe, s["x_loaded"], 32 * (b + 1))
                    need(pe, s["xft_sb"], b)
                    need(pe, s["v_sb"], b - 1)
                    for wt in range(WT):
                        for r in range(R):
                            last = nc.tensor.transpose(pair_tile(0, r * WT + wt), xin[:, wt, r * C:(r + 1) * C], ident[:, :])
                    last.then_inc(s["xt_ps"], 1)
                elif item == "conv":
                    pe.wait_ge(s["xt_sb"], b + 1)
                    for t in range(NT):
                        r, w0 = t // WT, (t % WT) * P
                        for i in range(TAPS):
                            c0 = w0 + (r + i) // R
                            last = nc.tensor.matmul(pair_tile(0, t), x_t[:, (r + i) % R, c0:c0 + P], conv_w(i),
                                                    start=(i == 0), stop=(i == TAPS - 1))
                    last.then_inc(s["conv_ps"], 1)
                elif item == "gram":
                    pe.wait_ge(s["x1_sb"], b + 1)
                    for t in range(NT):
                        last = nc.tensor.matmul(ps[:, 0, 0:C + 1], x1[0:ROWS[t], t, 0:C], x1[0:ROWS[t], t, :],
                                                start=(t == 0), stop=(t == NT - 1))
                    last.then_inc(s["gram_ps"], 1)
                elif item == "gram_v":
                    pe.wait_ge(s["gram_sb"], b + 1)
                    nc.tensor.matmul(ps[:, 1, 0:C], gram[:, :], wv0_t, start=True, stop=True).then_inc(s["gram_v_ps"], 1)
                elif item == "kv":
                    pe.wait_ge(s["gram_v_sb"], b + 1)
                    nc.tensor.matmul(ps[:, 0, 0:C], wth_t, gram_v[:, :], start=True, stop=True).then_inc(s["kv_ps"], 1)
                elif item == "x1t":
                    pe.wait_ge(s["kv_sb"], b + 1)
                    turn(0, x1).then_inc(s["x1t_ps"], 1)
                elif item == "attn":
                    pe.wait_ge(s["x1t_sb"], b + 1)
                    per_tile(0, [cols(x1_t), lambda t: x_mean[:, :]], [kv[:, :], wv0_t]).then_inc(s["attn_ps"], 1)
                elif item == "xrt":
                    pe.wait_ge(s["xr_sb"], b + 1)
                    turn(0, xr).then_inc(s["xrt_ps"], 1)
                elif item == "route":
                    pe.wait_ge(s["xrt_sb"], b + 1)
                    for t in range(NT):
                        last = nc.tensor.matmul(ps[:, 0, t * E0:(t + 1) * E0], cols(xr_t)(t), w_gate[:, :],
                                                start=(t == 0), stop=(t == NT - 1), skip_group_check=True)
                    last.then_inc(s["route_ps"], 1)
                else:
                    pe.wait_ge(s["comb_sb"], b + 1)
                    turn(0, xf).then_inc(s["xft_ps"], 1)

            def ffn(item, b):
                if item[0] == "up":
                    _, e, k = item
                    n = (HC * E0) * b + HC * e + k
                    if e == 0 and k == 0:
                        pe.wait_ge(s["xft_sb"], b + 1)
                    need(pe, s["hid_sb"], n - 1)
                    for r in range(R):
                        last = nc.tensor.matmul(ps[:, 2 + 2 * (k % 2) + r, 0:PITCH], w1[:, e, k * P:(k + 1) * P],
                                                xf_t[:, r * PITCH:(r + 1) * PITCH], start=True, stop=True)
                    last.then_inc(s["up_ps"], 1)
                elif item[0] == "down":
                    e = item[1]
                    pe.wait_ge(s["hid_sb"], HC * (E0 * b + e + 1))
                    need(pe, s["ffn_acc"], E0 * b + e)
                    for t in range(NT):
                        for k in range(HC):
                            last = nc.tensor.matmul(pair_tile(3, t), hid[e % 2][:, k, tile_cols(t):tile_cols(t) + P],
                                                    w2[:, e, k, :], start=(k == 0), stop=(k == HC - 1))
                    last.then_inc(s["down_ps"], 1)

            def back(item, b, pair_reader):
                if item == "x3t":
                    pe.wait_ge(s["x3_sb"], b + 1)
                    need(pe, s["xft_sb"], pair_reader)
                    turn(0, x3).then_inc(s["x3t_ps"], 1)
                elif item == "v":
                    need(pe, s["qk_split"], 4 * b + 4)
                    per_tile(0, [cols(x3_t)], [w_v[:, :]]).then_inc(s["v_ps"], 1)
                else:
                    n = int(item[2])
                    pe.wait_ge(s["x3t_sb"], b + 1)
                    if n:
                        pe.wait_ge(s["qk_split"], 4 * b + n)
                    for r in range(R):
                        last = nc.tensor.matmul(ps[:, r, 0:PITCH], w_qk[:, n, :], x3_t[:, r * PITCH:(r + 1) * PITCH],
                                                start=True, stop=True)
                    last.then_inc(s["qk_ps"], 1)

            def run(i, items):
                for kind, item in items:
                    if kind == "front":
                        front(item, i)
                    elif kind == "ffn":
                        ffn(item, i - 1)
                    else:
                        back(item, i - 2, i if not isinstance(i, int) or i < B else B)

            both = first_part(run)
            with pe.Fori(2, B) as i:
                run(i, both)
            run(B, plan(False, True, True))
            run(B + 1, plan(False, False, True))

            def row_scores(g, slot, t):
                j = g * SLOTS + slot
                if t == 0:
                    pe.wait_ge(stack_loaded[slot], 16 * 9 * (g + 1))
                n = NT * j + t
                need(pe, s["row_exp"], n - 1)
                m, c0 = ROWS[t], tile_cols(t)
                for r in range(R):
                    last = nc.tensor.matmul(ps[0:m, 2 * (t % 2) + r, 0:W], q_st[slot][0:SK, c0:c0 + m],
                                            k_st[slot][0:SK, r * PITCH:r * PITCH + W], start=True, stop=True)
                last.then_inc(s["row_scored"], 1)

            def turned_scores(g, slot, t):
                j = g * SLOTS + slot
                if t == 0:
                    pe.wait_ge(shift_loaded[slot], 16 * (g + 1))
                n = NT * j + t
                need(pe, s["t_exp"], n)
                m, c0 = ROWS[t], tile_cols(t)
                for r in range(R):
                    last = nc.tensor.matmul(ps[0:m, 4 + r, 0:W], k_st[slot][0:STACK, c0:c0 + m],
                                            q_st[slot][0:STACK, r * PITCH:r * PITCH + W], start=True, stop=True)
                last.then_inc(s["t_scored"], 1)

            def weighted_values(g, slot, kt):
                j = g * SLOTS + slot
                n = NT * j + kt
                bank = 6 + slot % 2
                if kt == 0:
                    if slot % 2 == 0:
                        pe.wait_ge(s["vh_ready"], 2 * g + slot // 2 + 1)
                    need(pe, s["o_copied"], j - 1)
                pe.wait_ge(s["t_exp"], n + 2)
                for k in (kt, kt + 1):
                    m = ROWS[k]
                    for r in range(R):
                        c = 32 * (R * (k % 2) + r)
                        last = nc.tensor.matmul(ps[c:c + VD, bank, 0:W], v_head[slot // 2][0:m, k, :],
                                                e_ring[n_slot(slot, k)][0:m, r, 0:W], start=(kt == 0), stop=(kt == NT - 2))
                last.then_inc(s["av_done"], 2)

            def turn_o(g, slot):
                pe.wait_ge(s["ot_sb"], g * SLOTS + slot + 1)
                for wt in range(WT):
                    q = ROWS[wt]
                    last = nc.tensor.matmul(ps[0:q, 6 + slot % 2, PITCH + wt * R * VD:PITCH + (wt + 1) * R * VD],
                                            o_t[slot % 2][0:OT_ROWS, wt * P:wt * P + q], pick[0:OT_ROWS, :],
                                            start=(wt == 0), stop=True, skip_group_check=True)
                last.then_inc(s["o_turned"], 1)

            def behind(g, n, first=False):
                n -= PE_LAG
                if first and n < 0:
                    return
                g, slot = (g, n // NT) if n >= 0 else (g - 1, n // NT + SLOTS)
                t = n % NT
                turned_scores(g, slot, t)
                very_first = first and slot == 0
                if t in (2, 4):
                    weighted_values(g, slot, t - 2)
                elif t == 0 and not very_first:
                    weighted_values(*earlier(g, slot, 1), NT - 2)
                elif t == 3 and not very_first:
                    turn_o(*earlier(g, slot, 1))

            pe.wait_ge(s["p1_done"], 1)
            for n in range(SLOTS * NT):
                row_scores(0, n // NT, n % NT)
                behind(0, n, True)
            with pe.Fori(1, BODIES) as g:
                for n in range(SLOTS * NT):
                    row_scores(g, n // NT, n % NT)
                    behind(g, n)
            for n in range(PE_LAG):
                behind(BODIES, n)
            weighted_values(BODIES - 1, SLOTS - 1, NT - 2)
            turn_o(BODIES - 1, SLOTS - 1)

            def third(b):
                pe.wait_ge(s["feat_ready"], b + 1)
                settle(pe, s["pe_passed"])
                for wt in range(WT):
                    last = nc.tensor.transpose(ps[0:H * 8, 0, wt * P:(wt + 1) * P],
                                               feat[:, wt].rearrange("p h m f -> p (h m f)"), ident[:, :])
                last.then_inc(s["feat_ps"], 1)
                pe.wait_ge(s["feat_sb"], b + 1)
                for i in range(2):
                    last = nc.tensor.matmul(ps[:, 2 + i, 0:PITCH], g1[:, i * P:(i + 1) * P], feat_t[:, :], start=True, stop=True)
                last.then_inc(s["g1_ps"], 1)
                pe.wait_ge(s["g1_sb"], b + 1)
                for i in range(2):
                    last = nc.tensor.matmul(ps[64 * i:64 * i + 64, 0, 0:PITCH], g2[:, :], hid1[:, i, :], start=True, stop=True)
                last.then_inc(s["g2_ps"], 1)
                pe.wait_ge(s["g2_sb"], b + 1)
                for wt in range(WT):
                    last = nc.tensor.matmul(ps[:, 2, wt * H:(wt + 1) * H], hid2[:, wt * P:(wt + 1) * P], g3[:, :],
                                            start=(wt == 0), stop=(wt == WT - 1), skip_group_check=True)
                last.then_inc(s["g3_ps"], 1)
                pe.wait_ge(s["fused"], b + 1)
                for t in range(NT):
                    last = nc.tensor.transpose(pair_tile(0, t), fo[0][:, t].rearrange("p h d -> p (h d)"), ident[:, :])
                last.then_inc(s["fused_ps"], 1)
                pe.wait_ge(s["fused_sb"], b + 1)
                per_tile(1, [cols(fo_t)], [w_o[:, :]]).then_inc(s["wo_ps"], 1)
                pe.wait_ge(s["x4_sb"], b + 1)
                turn(0, x4).then_inc(s["x4t_ps"], 1)
                pe.wait_ge(s["x4t_sb"], b + 1)
                for t in range(NT):
                    last = nc.tensor.matmul(ps[:, 2, t * E1:(t + 1) * E1], cols(x4_t)(t), sw_t[:, :],
                                            start=(t == 0), stop=(t == NT - 1), skip_group_check=True)
                last.then_inc(s["route1_ps"], 1)
                pe.wait_ge(s["onehot"], b + 1)
                for wt in range(WT + 1):
                    for u in range(min(wt + 1, WT)):
                        m = ROWS[u]
                        last = nc.tensor.matmul(ps[:, 3, wt * E1:(wt + 1) * E1],
                                                (before if u == wt else ones_bf)[0:m, :], ohs[0:m, u, :],
                                                start=(wt == 0 and u == 0), stop=(u == min(wt, WT - 1)), skip_group_check=True)
                last.then_inc(s["rank_ps"], 1)
                pe.wait_ge(s["mask_sb"], b + 1)
                settle(pe, s["pe_passed"])
                for t in range(NT):
                    last = nc.tensor.transpose(ps[0:E1, t // WT, (t % WT) * P:(t % WT + 1) * P], mask[:, t, :], ident[:, :])
                last.then_inc(s["mask_ps"], 1)
                pe.wait_ge(s["maskt_sb"], b + 1)
                for t in range(NT):
                    last = nc.tensor.matmul(pair_tile(1, t), mask_t[:, tile_cols(t):tile_cols(t) + P], ex_b[:, :],
                                            start=True, stop=True)
                last.then_inc(s["bias_ps"], 1)
                for t in range(NT):
                    for q in range(4):
                        n = 4 * t + q
                        need(pe, s["ex_used"], 4 * NT * b + n - 3)
                        nc.tensor.matmul(ps[:, 4 + q, :], cols(x4_t)(t),
                                         w_t[:, TAPS + 2 + 4 * q:TAPS + 6 + 4 * q, :].rearrange("p a b -> p (a b)"),
                                         start=True, stop=True).then_inc(s["ex_ps"], 1)

            third(0)
            with pe.Fori(1, B) as b:
                third(b)

        @block.scalar
        def _(act):
            def copy(dst, src, name, scale=1.0):
                nc.scalar.activation(dst, src, ACT.Copy, scale=scale).then_inc(s[name], 1)

            for n in range(N_NAT + 1):
                act.wait_ge(s["nat_ps"], n + 1)
                if n < N_NAT:
                    copy(w_t[:, n, :], ps[:, n % 8, 0:P], "nat_sb")
                else:
                    copy(sw_t[:, :], ps[:, n % 8, 0:E1], "nat_sb")

            def front(item, b):
                if item == "xt":
                    act.wait_ge(s["xt_ps"], b + 1)
                    need(act, s["conv_ps"], b)
                    copy(x_t[:, :, 0:PITCH], pair(0), "xt_sb")
                elif item == "gram":
                    act.wait_ge(s["gram_ps"], b + 1)
                    need(act, s["attn_ps"], b)
                    nc.scalar.activation(gram[:, :], ps[:, 0, 0:C], ACT.Copy)
                    copy(x_mean[:, :], ps[:, 0, C:C + 1].to_broadcast((P, P)), "gram_sb", 1.0 / L)
                elif item == "gram_v":
                    act.wait_ge(s["gram_v_ps"], b + 1)
                    copy(gram_v[:, :], ps[:, 1, 0:C], "gram_v_sb")
                elif item == "kv":
                    act.wait_ge(s["kv_ps"], b + 1)
                    copy(kv[:, :], ps[:, 0, 0:C], "kv_sb", 1.0 / (L * C ** 0.5))
                elif item == "x1t":
                    act.wait_ge(s["x1t_ps"], b + 1)
                    copy(as_pair(x1_t[:, :]), pair(0), "x1t_sb")
                elif item == "xrt":
                    act.wait_ge(s["xrt_ps"], b + 1)
                    need(act, s["route_ps"], b)
                    copy(as_pair(xr_t[:, :]), pair(0), "xrt_sb")
                elif item == "route":
                    act.wait_ge(s["logit_sb"], b + 1)
                    nc.scalar.activation(r_b[:, :, 0:E0], r_a[:, :, 0:E0], ACT.Exp).then_inc(s["exp_sb"], 1)
                elif item == "handover":
                    act.wait_ge(s["xft_ps"], b + 1)
                    need(act, s["down_ps"], E0 * b)
                    copy(as_pair(xf_t[:, :]), pair(0), "xft_sb", gamma[:, 0:1])

            def ffn(item, b):
                if item[0] == "up":
                    _, e, k = item
                    n = (HC * E0) * b + HC * e + k
                    act.wait_ge(s["up_ps"], n + 1)
                    if k == 0:
                        need(act, s["down_ps"], E0 * b + e - 1)
                    nc.scalar.activation(as_pair(hid[e % 2][:, k, :]), pair(1 + k % 2), ACT.Gelu).then_inc(s["hid_sb"], 1)

            def back(item, b):
                if item == "x3t":
                    act.wait_ge(s["x3t_ps"], b + 1)
                    need(act, s["v_ps"], b)
                    copy(as_pair(x3_t[:, :]), pair(0), "x3t_sb")
                elif item != "v":
                    n = int(item[2])
                    act.wait_ge(s["qk_ps"], 4 * b + n + 1)
                    need(act, parts_stored[n], 16 * H * b)
                    copy(as_pair(parts[:, n, 0, :]), pair(0), "part1_sb", 2.0 * HD ** -0.5 if n % 2 == 0 else 1.0)

            def run(i, items):
                for kind, item in items:
                    if kind == "front":
                        front(item, i)
                    elif kind == "ffn":
                        ffn(item, i - 1)
                    else:
                        back(item, i - 2)

            both = first_part(run)
            with act.Fori(2, B) as i:
                run(i, both)
            run(B, plan(False, True, True))
            run(B + 1, plan(False, False, True))

            def row_exp(j, slot, t):
                n = NT * j + t
                act.wait_ge(s["neg_max"], n + 1)
                need(act, s["min_done"], n - 3)
                if t == 0:
                    need(act, s["stat_saved"], j - SLOTS + 1)
                nc.scalar.activation(f_ring[(NT * slot + t) % 4][:, :, :], ps[:, 2 * (t % 2):2 * (t % 2) + 2, 0:W], ACT.Exp,
                                     bias=stat[slot][:, 0, t:t + 1],
                                     accum_out=stat[slot][:, 1, t:t + 1]).then_inc(s["row_exp"], 1)

            def turned_exp(j, slot, t):
                n = NT * j + t
                act.wait_ge(s["t_scored"], n + 1)
                need(act, s["av_done"], n - ERING + 1)
                nc.scalar.activation(e_ring[n_slot(slot, t)][:, :, 0:W], ps[:, 4:6, 0:W], ACT.Exp,
                                     scale=0.5).then_inc(s["t_exp"], 1)

            def copy_ot(j, slot):
                act.wait_ge(s["av_done"], NT * (j + 1))
                nc.scalar.activation(o_t[slot % 2][0:OT_ROWS, :], ps[0:OT_ROWS, 6 + slot % 2, 0:W], ACT.Copy).then_inc(s["ot_sb"], 1)

            def save_o(j, slot):
                act.wait_ge(s["o_turned"], j + 1)
                settle(act, s["act_passed"])
                nc.scalar.activation(o_all[:, bass.ds(j, 1), :].rearrange("p a (r w v) -> p (a r) w v", r=R, w=WT),
                                     ps[:, 6 + slot % 2, PITCH:PITCH + NT * VD].rearrange("p (w r v) -> p r w v", r=R, w=WT),
                                     ACT.Copy).then_inc(s["o_copied"], 1)

            def steps(g, first):
                for slot in range(SLOTS):
                    j = g * SLOTS + slot
                    for t in range(NT):
                        row_exp(j, slot, t)
                        if not (first and slot <= LAG):
                            if t == 1:
                                copy_ot(j - LAG - 1, (slot - LAG - 1) % SLOTS)
                            elif t == 5:
                                save_o(j - LAG - 1, (slot - LAG - 1) % SLOTS)
                        if not (first and slot < LAG):
                            turned_exp(j - LAG, (slot - LAG) % SLOTS, t)

            steps(0, True)
            with act.Fori(1, BODIES) as g:
                steps(g, False)
            for j in range(STEPS - LAG, STEPS):
                for t in range(NT):
                    turned_exp(j, j % SLOTS, t)
                    if t == 1:
                        copy_ot(j - 1, (j - 1) % SLOTS)
                    elif t == 5:
                        save_o(j - 1, (j - 1) % SLOTS)
            copy_ot(STEPS - 1, SLOTS - 1)
            save_o(STEPS - 1, SLOTS - 1)

            def third(b):
                act.wait_ge(s["feat_ps"], b + 1)
                copy(feat_t[:, :], ps[0:H * 8, 0, 0:PITCH], "feat_sb")
                act.wait_ge(s["g1_ps"], b + 1)
                nc.scalar.activation(hid1[:, :, :], ps[:, 2:4, 0:PITCH], ACT.Relu, bias=gb1[:, 0:1]).then_inc(s["g1_sb"], 1)
                act.wait_ge(s["g2_ps"], b + 1)
                nc.scalar.activation(hid2[:, :], ps[:, 0, 0:PITCH], ACT.Relu, bias=gb2[:, 0:1]).then_inc(s["g2_sb"], 1)
                act.wait_ge(s["g3_ps"], b + 1)
                nc.scalar.activation(alpha[:, :, :].rearrange("p w h -> p (w h)"), ps[:, 2, 0:WT * H], ACT.Exp,
                                     scale=-1.0, bias=ngb3[:, 0:1]).then_inc(s["g3_sb"], 1)
                act.wait_ge(s["fused_ps"], b + 1)
                copy(as_pair(fo_t[:, :]), pair(0), "fused_sb")
                act.wait_ge(s["x4t_ps"], b + 1)
                need(act, s["ex_ps"], 4 * NT * b)
                copy(as_pair(x4_t[:, :]), pair(0), "x4t_sb")
                act.wait_ge(s["logit1_sb"], b + 1)
                nc.scalar.activation(r_b[:, :, :], r_a[:, :, :], ACT.Exp).then_inc(s["exp1_sb"], 1)
                act.wait_ge(s["mask_ps"], b + 1)
                copy(as_pair(mask_t[:, :]), ps[0:E1, 0:2, 0:PITCH], "maskt_sb")

            third(0)
            with act.Fori(1, B) as b:
                third(b)

        @block.gpsimd
        def _(pool):
            nc.gpsimd.memset(ident[:, :], 0.0).then_inc(s["pool_step"], 1)
            nc.gpsimd.memset(before[:, :], 1.0).then_inc(s["pool_step"], 1)
            nc.gpsimd.memset(ones_bf[:, :], 1.0)
            nc.gpsimd.memset(minus_half[:, :], -0.5)
            nc.gpsimd.memset(plus_half[:, :], 0.5)
            for i in range(2):
                nc.gpsimd.memset(mp[i][:, :], 0.0)
            nc.gpsimd.iota(rank_desc[:, :], pattern=[[-1, E1]], base=E1, channel_multiplier=0,
                           allow_small_or_imprecise_dtypes=True)
            pool.wait_ge(s["pool_step"], 2)
            nc.gpsimd.affine_select(out=before[:, :], in_=before[:, :], compare_op=ALU.is_gt, fill=0.0,
                                    base=0, pattern=[[1, P]], channel_multiplier=-1).then_inc(s["pool_step"], 1)
            nc.gpsimd.affine_select(out=ident[:, :], in_=ident[:, :], compare_op=ALU.not_equal, fill=1.0,
                                    base=0, pattern=[[-1, P]], channel_multiplier=1).then_inc(s["pool_step"], 1)
            nc.gpsimd.memset(pick[:, :], 0.0).then_inc(s["pool_step"], 1)
            for c in range(2 * R):
                pool.wait_ge(s["pool_step"], 5 + c)
                half = pick[:, (c % R) * VD:(c % R + 1) * VD]
                nc.gpsimd.affine_select(out=half, in_=half, compare_op=ALU.not_equal, fill=1.0,
                                        base=-32 * c, pattern=[[-1, VD]], channel_multiplier=1).then_inc(s["pool_step"], 1)
            pool.wait_ge(s["pool_step"], 9)
            pool.wait_ge(s["const_ready"], 1)
            pool.wait_ge(s["w_loaded"], N_WLOAD)
            nc.gpsimd.tensor_scalar(ngb3[:, :], gb3[:, :], -1.0, 0.0, ALU.mult, ALU.add).then_inc(s["const_ready"], 1)

            def norm(n):
                pool.wait_ge(s["var_ready"], n + 1)
                nc.gpsimd.tensor_tensor(rstd[:, :], var_eps[:, :], minus_half[:, 0:1].to_broadcast((P, NT)),
                                        ALU.pow).then_inc(s["rstd_ready"], 1)

            def run(i, items):
                n = 0
                for kind, item in items:
                    if item in ("conv", "attn", "route") or (kind == "back" and item == "x3t"):
                        norm(norm_base(i) + n)
                        n += 1
                    if item == ("end",):
                        pool.wait_ge(s["h2_sb"], i)
                        settle(pool, s["pool_passed"])
                        nc.gpsimd.tensor_copy(h_all[:, bass.ds(i - 1, 1), :].rearrange("p a c -> p (a c)"),
                                              h_two[:, :, :].rearrange("p t c -> p (t c)")).then_inc(s["h_stored"], 1)

            both = first_part(run)
            with pool.Fori(2, B) as i:
                run(i, both)
            run(B, plan(False, True, True))
            run(B + 1, plan(False, False, True))

            def steps(g, first):
                for slot in range(SLOTS):
                    j = g * SLOTS + slot
                    if slot % 2 == 0:
                        bh = 2 * g + slot // 2
                        need(pool, s["av_done"], 2 * NT * (bh - 1))
                        settle(pool, s["pool_passed"])
                        nc.gpsimd.tensor_copy(
                            v_head[slot // 2][:, :, :],
                            v_all[:, bass.ds(g // (H // 2), 1), :, :].rearrange("p a (t h) d -> p (a t) h d", h=H)
                            [:, :, bass.ds((g % (H // 2)) * 2 + slot // 2, 1), :].rearrange("p t a d -> p t (a d)")
                        ).then_inc(s["vh_ready"], 1)
                    pool.wait_ge(s["neg_max"], NT * (j + 1))
                    need(pool, s["max_turned"], j - 1)
                    a = mp[slot % 2]
                    settle(pool, s["pool_passed"])
                    base = 4 * j + 9
                    nc.gpsimd.tensor_copy(a[:, 0:NT], stat[slot][:, 0, :]).then_inc(s["pool_step"], 1)
                    pool.wait_ge(s["pool_step"], base + 1)
                    nc.gpsimd.tensor_tensor(mp_r[:, 0, :], stat[slot][:, 0, :], a[:, 0:NT], ALU.subtract).then_inc(s["pool_step"], 1)
                    pool.wait_ge(s["pool_step"], base + 2)
                    settle(pool, s["pool_passed"])
                    nc.gpsimd.tensor_copy(a[:, NT:2 * NT], mp_r[:, 0, :]).then_inc(s["pool_step"], 1)
                    pool.wait_ge(s["pool_step"], base + 3)
                    nc.gpsimd.tensor_tensor(mp_r[:, 1, :], mp_r[:, 0, :], a[:, NT:2 * NT], ALU.subtract).then_inc(s["pool_step"], 1)
                    pool.wait_ge(s["pool_step"], base + 4)
                    settle(pool, s["pool_passed"])
                    nc.gpsimd.tensor_copy(a[:, 2 * NT:3 * NT], mp_r[:, 1, :]).then_inc(s["max_parts"], 1)
                    pool.wait_ge(s["max_parts"], j + 1)
                    if not (first and slot == 0):
                        save_stat(j - 1, (slot - 1) % SLOTS)

            def save_stat(j, slot):
                pool.wait_ge(s["row_exp"], NT * (j + 1))
                pool.wait_ge(s["min_done"], NT * (j + 1))
                settle(pool, s["pool_passed"])
                nc.gpsimd.tensor_copy(stat_all[:, bass.ds(j, 1), :].rearrange("p a c -> p (a c)"),
                                      stat[slot][:, :, :].rearrange("p a c -> p (a c)")).then_inc(s["stat_saved"], 1)

            steps(0, True)
            with pool.Fori(1, BODIES) as g:
                steps(g, False)
            save_stat(STEPS - 1, SLOTS - 1)

            def third(b):
                pool.wait_ge(s["pow_in"], b + 1)
                nc.gpsimd.tensor_tensor(pw_out[:, :, :], pw_in[:, :, :],
                                        plus_half[:, 0:1].unsqueeze(2).to_broadcast((P, 2, H * 2 * NT)),
                                        ALU.pow).then_inc(s["pow_out"], 1)
                norm(NLN0 * B + b)

            third(0)
            with pool.Fori(1, B) as b:
                third(b)

        @block.vector
        def _(dve):
            nc.vector.memset(ps[:, :, :], 0.0)
            nc.vector.memset(x_t[:, :, :], 0.0)
            nc.vector.memset(x1[:, :, :], 1.0)
            nc.vector.memset(v_all[:, :, :, :].rearrange("p a b c -> p (a b c)"), 1.0)
            nc.vector.memset(carry[:, :], 0.0)
            nc.vector.memset(g1[:, :], 0.0)
            nc.vector.memset(g2[:, :], 0.0)
            nc.vector.memset(g3[:, :], 0.0)
            nc.vector.memset(xin[:, :, :], 0.0).then_inc(s["const_ready"], 1)

            def norm(c, n, src, dst, name):
                for t in range(NT):
                    last = nc.vector.bn_stats(bn[:, t, :], src[:, t, 0:C])
                c.link(last)
                settle(dve, s["dve_passed"])
                for t in range(NT):
                    last = nc.vector.bn_aggr(mv[:, t, :], bn[:, t, :])
                c.link(last)
                nc.vector.tensor_scalar(var_eps[:, :], mv[:, :, 1], LN_EPS, None, ALU.add).then_inc(s["var_ready"], 1)
                dve.wait_ge(s["rstd_ready"], n + 1)
                for t in range(NT):
                    last = nc.vector.tensor_scalar(dst[:, t, 0:C], src[:, t, 0:C], mv[:, t, 0:1], rstd[:, t:t + 1],
                                                   ALU.subtract, ALU.mult)
                last.then_inc(s[name], 1)

            def bc(ap, n):
                return ap.unsqueeze(2).to_broadcast((P, NT, n))

            def soft(c, sem_in, sem_out, value, n, logits):
                c.link(nc.vector.tensor_reduce(r_m[:, :], r_c[:, :, 0:n], X_AXIS, ALU.max))
                nc.vector.tensor_tensor(r_a[:, :, 0:n], r_c[:, :, 0:n], bc(r_m[:, :], n), ALU.subtract).then_inc(s[sem_in], 1)
                dve.wait_ge(s[sem_out], value)
                c.link(nc.vector.tensor_reduce(r_n[:, :], r_b[:, :, 0:n], X_AXIS, ALU.add))
                c.link(nc.vector.reciprocal(r_g[:, :], r_n[:, :]))
                c.link(nc.vector.tensor_tensor(r_p[:, :, 0:n], r_b[:, :, 0:n], bc(r_g[:, :], n), ALU.mult))
                c.link(nc.vector.tensor_reduce(r_m[:, :], r_p[:, :, 0:n], X_AXIS, ALU.max))
                c.link(nc.vector.tensor_tensor(r_a[:, :, 0:n], r_p[:, :, 0:n], bc(r_m[:, :], n), ALU.is_equal))
                c.link(nc.vector.tensor_tensor(r_c[:, :, 0:n], r_a[:, :, 0:n],
                                               rank_desc[:, 0:n].unsqueeze(1).to_broadcast((P, NT, n)), ALU.mult))
                c.link(nc.vector.tensor_reduce(r_n[:, :], r_c[:, :, 0:n], X_AXIS, ALU.max))
                c.link(nc.vector.tensor_tensor(oh[:, :, 0:n], r_c[:, :, 0:n], bc(r_n[:, :], n), ALU.is_equal))

            def front(item, b, c, n):
                if item == "conv":
                    dve.wait_ge(s["conv_ps"], b + 1)
                    if not (isinstance(b, int) and b == 0):
                        dve.wait_ge(s["comb_sb"], b)
                    c.link(nc.vector.tensor_tensor(
                        h_cur[:, :, :].rearrange("p (r w) c -> p r w c", r=R),
                        pair(0).rearrange("p r (w c) -> p r w c", c=C),
                        conv_b[:, :].unsqueeze(1).unsqueeze(1).to_broadcast((P, R, WT, C)), ALU.add))
                    c.link(nc.vector.tensor_scalar(h_cur[:, :, :], h_cur[:, :, :], 0.0, None, ALU.max))
                    norm(c, n, h_cur, x1, "x1_sb")
                elif item == "attn":
                    dve.wait_ge(s["attn_ps"], b + 1)
                    c.link(nc.vector.tensor_tensor(as_pair(h_cur[:, :, :]), as_pair(h_cur[:, :, :]), pair(0), ALU.add))
                    norm(c, n, h_cur, xr, "xr_sb")
                elif item == "route":
                    dve.wait_ge(s["xr_sb"], b + 1)
                    norm(c, n, xr, xf, "xf_sb")
                    dve.wait_ge(s["route_ps"], b + 1)
                    c.link(nc.vector.tensor_copy(r_c[:, :, 0:E0], ps[:, 0, 0:NT * E0].rearrange("p (t e) -> p t e", e=E0)))
                    soft(c, "logit_sb", "exp_sb", b + 1, E0, None)
                    c.link(nc.vector.tensor_tensor(r_a[:, :, 0:E0], r_p[:, :, 0:E0], oh[:, :, 0:E0], ALU.mult))
                    c.link(nc.vector.tensor_tensor(r_c[:, :, 0:E0], r_p[:, :, 0:E0], r_a[:, :, 0:E0], ALU.subtract))
                    c.link(nc.vector.tensor_reduce(r_n[:, :], r_c[:, :, 0:E0], X_AXIS, ALU.max))
                    c.link(nc.vector.scalar_tensor_tensor(r_n[:, :], r_m[:, :], GATE_EPS, r_n[:, :], ALU.add, ALU.add))
                    c.link(nc.vector.reciprocal(r_g[:, :], r_n[:, :]))
                    c.link(nc.vector.tensor_tensor(r_n[:, :], r_m[:, :], r_g[:, :], ALU.mult))
                    c.link(nc.vector.tensor_tensor(comb_next[:, :, :], oh[:, :, 0:E0], bc(r_n[:, :], E0), ALU.mult))
                elif item == "handover":
                    need(dve, s["h2_sb"], b)
                    c.link(nc.vector.tensor_copy(h_acc[:, :, :], h_cur[:, :, :]))
                    nc.vector.tensor_copy(comb[:, :, :], comb_next[:, :, :]).then_inc(s["comb_sb"], 1)

            def ffn(item, b, c):
                if item[0] == "down":
                    e = item[1]
                    dve.wait_ge(s["down_ps"], E0 * b + e + 1)
                    if e == 0:
                        dve.wait_ge(s["comb_sb"], b + 1)
                    else:
                        dve.wait_ge(s["ffn_acc"], E0 * b + e)
                    for t in range(NT):
                        last = nc.vector.scalar_tensor_tensor(h_acc[:, t, :], pair_tile(3, t), comb[:, t, e:e + 1], h_acc[:, t, :],
                                                              ALU.mult, ALU.add)
                    last.then_inc(s["ffn_acc"], 1)
                elif item[0] == "end":
                    dve.wait_ge(s["ffn_acc"], E0 * (b + 1))
                    need(dve, s["h_stored"], b)
                    nc.vector.tensor_copy(h_two[:, :, :], h_acc[:, :, :]).then_inc(s["h2_sb"], 1)

            def back(item, b, c, n):
                if item == "x3t":
                    dve.wait_ge(s["h2_sb"], b + 1)
                    norm(c, n, h_two, x3, "x3_sb")
                elif item == "v":
                    dve.wait_ge(s["v_ps"], b + 1)
                    settle(dve, s["dve_passed"])
                    nc.vector.tensor_copy(
                        v_all[:, bass.ds(b, 1), :, 0:HD].rearrange("p a (r k) d -> p (a r) k d", r=R),
                        pair(0).rearrange("p r (k d) -> p r k d", d=HD)).then_inc(s["v_sb"], 1)
                else:
                    k = int(item[2])
                    dve.wait_ge(s["part1_sb"], 4 * b + k + 1)
                    c.link(nc.vector.scalar_tensor_tensor(as_pair(rest[:, :]), pair(0), 2.0 * HD ** -0.5 if k % 2 == 0 else 1.0,
                                                          as_pair(parts[:, k, 0, :]), ALU.mult, ALU.subtract))
                    c.link(nc.vector.tensor_copy(parts[:, k, 1, :], rest[:, :]))
                    nc.vector.tensor_tensor(parts[:, k, 2, :], rest[:, :], parts[:, k, 1, :], ALU.subtract).then_inc(s["qk_split"], 1)

            STEADY = 37
            BACK_N = 10
            FRONT_N = STEADY - BACK_N

            def run(i, items):
                if isinstance(i, int):
                    base = FRONT_N * min(i, B) + BACK_N * max(0, i - 2)
                else:
                    base = STEADY * i - 2 * BACK_N
                c = Chain(dve, s["dve_step"], base)
                n = 0
                for kind, item in items:
                    if kind == "front":
                        front(item, i, c, norm_base(i) + n)
                        n += item in ("conv", "attn", "route")
                    elif kind == "ffn":
                        ffn(item, i - 1, c)
                    else:
                        back(item, i - 2, c, norm_base(i) + n)
                        n += item == "x3t"
                fronts = any(k == "front" for k, _ in items)
                backs = any(k == "back" for k, _ in items)
                assert c.n == FRONT_N * fronts + BACK_N * backs, (c.n, fronts, backs)

            both = first_part(run)
            with dve.Fori(2, B) as i:
                run(i, both)
            run(B, plan(False, True, True))
            run(B + 1, plan(False, False, True))
            first_steps = FRONT_N * B + BACK_N * B
            dve.wait_ge(s["v_sb"], B)
            for n in range(4):
                dve.wait_ge(parts_stored[n], 16 * H * B)
            for i in range(SLOTS):
                last = nc.vector.memset(k_st[i][SHIFT0:STACK, :], 1.0)
            last.then_inc(s["p1_done"], 1)

            def row_max(j, slot, t):
                n = NT * j + t
                dve.wait_ge(s["row_scored"], n + 1)
                if t == 0:
                    need(dve, s["stat_saved"], j - SLOTS + 1)
                nc.vector.tensor_reduce(stat[slot][:, 0, t:t + 1], ps[:, 2 * (t % 2):2 * (t % 2) + 2, 0:W],
                                        XY_AXES, ALU.max, negate=True).then_inc(s["neg_max"], 1)

            def row_min(j, slot, t):
                n = NT * j + t
                dve.wait_ge(s["row_exp"], n + 1)
                nc.vector.tensor_reduce(stat[slot][:, 2, t:t + 1], f_ring[(NT * slot + t) % 4][:, :, :],
                                        XY_AXES, ALU.min).then_inc(s["min_done"], 1)

            def turn_max(j, slot):
                dve.wait_ge(s["max_parts"], j + 1)
                nc.vector.transpose(mp_t[slot][:, :], mp[slot % 2][:, :]).then_inc(s["max_turned"], 1)

            def steps(g, first):
                for slot in range(SLOTS):
                    j = g * SLOTS + slot
                    for t in range(NT):
                        row_max(j, slot, t)
                        if t == 1 and not (first and slot == 0):
                            turn_max(j - 1, (slot - 1) % SLOTS)
                        n = NT * slot + t - 2
                        if first and n < 0:
                            continue
                        row_min(g * SLOTS + n // NT, (n // NT) % SLOTS, n % NT)

            steps(0, True)
            with dve.Fori(1, BODIES) as g:
                steps(g, False)
            turn_max(STEPS - 1, SLOTS - 1)
            for t in range(NT - 2, NT):
                row_min(STEPS - 1, SLOTS - 1, t)

            def third(b, first):
                c = Chain(dve, s["dve_step"], first_steps + THIRD_N * b)
                if first:
                    dve.wait_ge(s["stat_saved"], STEPS)
                    dve.wait_ge(s["o_copied"], STEPS)
                settle(dve, s["dve_passed"])
                ob = o_all[:, bass.ds(b * H * 2, H * 2), :].rearrange("p k (t v) -> p k t v", v=VD)
                st = stat_all[:, bass.ds(b * H * 2, H * 2), :].rearrange("p k (q t) -> p k q t", t=NT)
                c.mark(nc.vector.tensor_copy(sum_p[:, :, :], ob[:, :, :, HD]))
                c.mark(nc.vector.tensor_copy(sq_p[:, :, :], st[:, :, 1, :]))
                c.link(nc.vector.tensor_copy(pw_in[:, 1, :].rearrange("p (k t) -> p k t", t=NT), st[:, :, 2, :]))
                c.link(nc.vector.tensor_scalar(sum_p[:, :, :], sum_p[:, :, :], 0.5, None, ALU.max))
                c.link(nc.vector.reciprocal(inv_s[:, :, :], sum_p[:, :, :]))
                c.mark(nc.vector.tensor_tensor(sum_p[:, :, :], sum_p[:, :, :], inv_s[:, :, :], ALU.mult))
                c.link(nc.vector.tensor_tensor(sq_p[:, :, :], sq_p[:, :, :], inv_s[:, :, :], ALU.mult))
                var = pw_in[:, 0, :].rearrange("p (k t) -> p k t", t=NT)
                c.mark(nc.vector.tensor_tensor(var, sum_p[:, :, :], sum_p[:, :, :], ALU.mult))
                c.link(nc.vector.tensor_tensor(sq_p[:, :, :], sq_p[:, :, :], inv_s[:, :, :], ALU.mult))
                c.link(nc.vector.scalar_tensor_tensor(var, var, -1.0 / L, sq_p[:, :, :], ALU.mult, ALU.add))
                nc.vector.tensor_scalar(var, var, 0.0, 1.0 / (L - 1), ALU.max, ALU.mult).then_inc(s["pow_in"], 1)
                dve.wait_ge(s["pow_out"], b + 1)
                low = pw_out[:, 1, :].rearrange("p (k t) -> p k t", t=NT)
                std = pw_out[:, 0, :].rearrange("p (k t) -> p k t", t=NT)
                c.link(nc.vector.tensor_tensor(low, low, inv_s[:, :, :], ALU.mult))
                for f, src in enumerate((sum_p[:, :, :], std, inv_s[:, :, :], low)):
                    fv = feat[:, :, :, :, f].rearrange("p w h m -> p w (h m)")
                    c.mark(nc.vector.tensor_tensor(fv, src[:, :, 0:WT].rearrange("p k w -> p w k"),
                                                   src[:, :, WT:NT].rearrange("p k w -> p w k"), ALU.add))
                c.sync()
                fm = feat[:, :, :, :, :].rearrange("p w h m f -> p (w h m) f")
                c.link(nc.vector.tensor_scalar(fm[:, :, 0], fm[:, :, 0], 1.0 / L, None, ALU.mult))
                nc.vector.tensor_scalar(feat[:, :, :, :, :].rearrange("p w h m f -> p (w h m f)"),
                                        feat[:, :, :, :, :].rearrange("p w h m f -> p (w h m f)"), 0.5, None, ALU.mult
                                        ).then_inc(s["feat_ready"], 1)
                dve.wait_ge(s["g3_sb"], b + 1)
                c.link(nc.vector.tensor_scalar(beta[:, :, :], alpha[:, :, :], 1.0, None, ALU.add))
                c.link(nc.vector.reciprocal(alpha[:, :, :], beta[:, :, :]))
                c.link(nc.vector.tensor_scalar(beta[:, :, :], alpha[:, :, :], -1.0, 1.0, ALU.mult, ALU.add))
                inv = inv_s[:, :, :].rearrange("p (h m) t -> p m h t", m=2)
                for m, a in enumerate((alpha, beta)):
                    for r in range(R):
                        c.mark(nc.vector.tensor_tensor(coef[:, m, :, r * WT:(r + 1) * WT], inv[:, m, :, r * WT:(r + 1) * WT],
                                                       a[:, :, :].rearrange("p w h -> p h w"), ALU.mult))
                c.sync()
                settle(dve, s["dve_passed"])
                for m in range(2):
                    c.mark(nc.vector.tensor_tensor(
                        fo[m][:, :, :, :].rearrange("p t h d -> p h t d"),
                        ob.rearrange("p (h m) t v -> p m h t v", m=2)[:, m, :, :, 0:HD],
                        coef[:, m, :, :].unsqueeze(3).to_broadcast((P, H, NT, HD)), ALU.mult))
                c.sync()
                nc.vector.tensor_tensor(fo[0][:, :, :, :], fo[0][:, :, :, :], fo[1][:, :, :, :], ALU.add).then_inc(s["fused"], 1)
                dve.wait_ge(s["wo_ps"], b + 1)
                settle(dve, s["dve_passed"])
                c.link(nc.vector.tensor_tensor(as_pair(h3[:, :, :]),
                                               h_all[:, bass.ds(b, 1), :].rearrange("p a (r c) -> p (a r) c", r=R),
                                               pair(1), ALU.add))
                norm(c, NLN0 * B + b, h3, x4, "x4_sb")
                dve.wait_ge(s["route1_ps"], b + 1)
                c.link(nc.vector.tensor_tensor(r_c[:, :, :], ps[:, 2, 0:NT * E1].rearrange("p (t e) -> p t e", e=E1),
                                               sw_b[:, :].unsqueeze(1).to_broadcast((P, NT, E1)), ALU.add))
                soft(c, "logit1_sb", "exp1_sb", b + 1, E1, None)
                nc.vector.tensor_tensor(ohs[:, :, :], oh[:, 0:WT, :], oh[:, WT:NT, :], ALU.add).then_inc(s["onehot"], 1)
                dve.wait_ge(s["rank_ps"], b + 1)
                rk = ps[:, 3, 0:(WT + 1) * E1].rearrange("p (w e) -> p w e", e=E1)
                c.link(nc.vector.tensor_tensor(r_a[:, 0:WT, :], rk[:, 0:WT, :],
                                               carry[:, :].unsqueeze(1).to_broadcast((P, WT, E1)), ALU.add))
                c.mark(nc.vector.tensor_tensor(carry[:, :], rk[:, WT, :], carry[:, :], ALU.add))
                c.link(nc.vector.tensor_tensor(r_a[:, WT:NT, :], r_a[:, 0:WT, :], oh[:, 0:WT, :], ALU.add))
                c.link(nc.vector.tensor_tensor(r_c[:, :, :], r_a[:, :, :], oh[:, :, :], ALU.mult))
                c.link(nc.vector.tensor_reduce(r_n[:, :], r_c[:, :, :], X_AXIS, ALU.add))
                c.link(nc.vector.tensor_scalar(r_n[:, :], r_n[:, :], float(CAPACITY), None, ALU.is_lt))
                c.link(nc.vector.tensor_tensor(r_g[:, :], r_n[:, :], r_m[:, :], ALU.mult))
                c.mark(nc.vector.tensor_tensor(self_c[:, :], r_m[:, :], r_g[:, :], ALU.subtract))
                nc.vector.tensor_tensor(mask[:, :, :], oh[:, :, :], bc(r_g[:, :], E1), ALU.mult).then_inc(s["mask_sb"], 1)
                c.sync()
                if not first:
                    dve.wait_ge(s["y_stored"], 16 * WT * b)
                for t in range(NT):
                    c.mark(nc.vector.scalar_tensor_tensor(y[:, t, :], x4[:, t, :], self_c[:, t:t + 1], h3[:, t, :], ALU.mult, ALU.add))
                c.sync()
                dve.wait_ge(s["bias_ps"], b + 1)
                c.link(nc.vector.tensor_tensor(as_pair(y[:, :, :]), as_pair(y[:, :, :]), pair(1), ALU.add))
                for t in range(NT):
                    for q in range(4):
                        dve.wait_ge(s["ex_ps"], 4 * NT * b + 4 * t + q + 1)
                        for e in range(4 * q, 4 * q + 4):
                            ins = nc.vector.scalar_tensor_tensor(y[:, t, :], ps[:, 4 + q, (e % 4) * P:(e % 4 + 1) * P],
                                                                 mask[:, t, e:e + 1], y[:, t, :], ALU.mult, ALU.add)
                            if e % 4 == 3:
                                ins.then_inc(s["ex_used"], 1)
                                dve.wait_ge(s["ex_used"], 4 * NT * b + 4 * t + q + 1)
                            else:
                                c.link(ins)
                nc.vector.tensor_copy(r_n[:, :], r_m[:, :]).then_inc(s["y_ready"], 1)
                assert c.n == THIRD_N, c.n

            THIRD_N = 125
            third(0, True)
            with dve.Fori(1, B) as b:
                third(b, False)


_INS = ['x', 'L0_tok_W', 'L0_tok_b', 'L0_attn_W_v', 'L0_attn_W_theta', 'L0_ffn_w_gating', 'L0_ffn_gamma', 'L0_ffn_w1',
        'L0_ffn_w2', 'L1_attn_Wq1', 'L1_attn_Wk1', 'L1_attn_Wq2', 'L1_attn_Wk2', 'L1_attn_Wv', 'L1_attn_Wo', 'L1_attn_gw1',
        'L1_attn_gb1', 'L1_attn_gw2', 'L1_attn_gb2', 'L1_attn_gw3', 'L1_attn_gb3', 'L1_ffn_switch_w', 'L1_ffn_switch_b',
        'L1_ffn_expert_w', 'L1_ffn_expert_b']


def kernel(**inputs):
    import numpy as _np
    import concourse.bacc as _bacc
    from concourse import mybir as _mybir
    from concourse.bass_utils import run_bass_kernel_spmd as _run

    nc = _bacc.Bacc("TRN2", target_bir_lowering=False, num_devices=1)
    arrays, args = {}, []
    for name in _INS:
        a = _np.ascontiguousarray(inputs[name])
        arrays[f"in_{name}"] = a
        args.append(nc.dram_tensor(f"in_{name}", a.shape, _mybir.dt.from_np(a.dtype), kind="ExternalInput").ap())
    args.append(nc.dram_tensor("out_0", (B, L, C), F32, kind="ExternalOutput").ap())
    build(nc, *args)
    r = _run(nc, [arrays], core_ids=[0])
    return r.results[0]["out_0"]
```

```python
from contextlib import ExitStack

import concourse.bass as bass
from concourse import mybir

F32 = mybir.dt.float32
BF16 = mybir.dt.bfloat16
ALU = mybir.AluOpType
ACT = mybir.ActivationFunctionType
X_AXIS = mybir.AxisListType.X
XY_AXES = mybir.AxisListType.XY

P = 128
B = 8
T_IN = 750
C = 128
TAPS = 5
L = T_IN - (TAPS - 1)
R = 2
W = L // R
WT = 3
NT = R * WT
PITCH = WT * P
N_LAST = W - (WT - 1) * P
ROWS = [P, P, N_LAST] * R
N_ALL = R * PITCH
W_IN = T_IN // R

E0 = 6
HID = 512
HC = HID // P
H = 8
HD = C // H
VD = HD + 1
PARTS = 3
TERMS = PARTS * (PARTS + 1) // 2
SK = TERMS * HD
SHIFT0 = SK
STACK = SK + PARTS
SLOTS = 4
STEPS = B * H * 2
BODIES = STEPS // SLOTS
ERING = 4
LAG = 2
PE_LAG = LAG * NT + 1
OT_ROWS = 3 * 32 + VD
E1 = 16
CAPACITY = int(1.2 * B * L / E1)
LN_EPS = 1e-5
GATE_EPS = 1e-9
GH1 = 32
GH2 = 16
NST = 3
NLN0 = 4


def tile_cols(t):
    return (t // WT) * PITCH + (t % WT) * P


def need(eng, sem, value):
    if isinstance(value, int) and value <= 0:
        return
    eng.wait_ge(sem, value)


def settle(eng, passed):
    eng.sem_inc(passed, 1)


class Chain:

    def __init__(self, eng, sem, base):
        self.eng, self.sem, self.base, self.n = eng, sem, base, 0

    def mark(self, ins):
        ins.then_inc(self.sem, 1)
        self.n += 1

    def sync(self):
        self.eng.wait_ge(self.sem, self.base + self.n)

    def link(self, ins):
        self.mark(ins)
        self.sync()


def norm_base(i):
    if isinstance(i, int):
        return 3 * min(i, B) + max(0, i - 2)
    return i * NLN0 - 2


def n_slot(slot, kt):
    return (NT * slot + kt) % ERING


def earlier(g, slot, lag):
    return (g, slot - lag) if slot >= lag else (g - 1, slot - lag + SLOTS)


def ffn_pieces():
    def down(e):
        return [("down", e, t) for t in range(NT)]
    out = []
    for e in range(E0):
        out += [("up", e, 0), ("up", e, 1)]
        if e:
            out += down(e - 1)
        out += [("up", e, 2), ("up", e, 3)]
    return out + down(E0 - 1)


FRONT = [("xt", 24), ("conv", 25), ("gram", 33), ("gram_v", 34), ("kv", 35), ("x1t", 36), ("attn", 38), ("xrt", 45), ("route", 48), ("xft", 55)]
BACK = [("x3n", 0), ("x3t", 7), ("qk0", 8), ("qk1", 12), ("qk2", 16), ("qk3", 20), ("v", 23)]


def plan(front, ffn, back):
    out = [(n, "back", x) for x, n in BACK] * back + [(n, "front", x) for x, n in FRONT] * front
    out += [(n + 0.5, "ffn", x) for n, x in enumerate(ffn_pieces())] * ffn
    out = [(kind, x) for _, kind, x in sorted(out, key=lambda item: item[0])]
    if ffn:
        out.append(("ffn", ("end",)))
    if front:
        out.append(("front", "handover"))
    return out


CHAIN = ["feat", "g1", "g2", "g3", "fuse", "wo", "x4", "stats", "route", "pick", "mask", "bias"]
PIECES_AFTER = [1, 1, 1, 1, 2, 2, 1, 0, 1, 1, 1, 0]
LEAD = 1
PIECES = 2 * NT


def piece(k):
    return [(2 * (k // 4) + i, k % 4, 4 + (2 * k + i) % 4) for i in range(2)]


SHARED = [1, 3, 5, 7]
ADD_AT = [3, 5, 7, 9]
PIECE_OPS, ADD_OPS = [], []
for _k in range(PIECES):
    PIECE_OPS.append((PIECE_OPS[-1] if PIECE_OPS else 0) + (0 if _k in SHARED else 8))
    if _k in ADD_AT:
        PIECE_OPS[-1] += 1
        ADD_OPS.append(PIECE_OPS[-1])
BATCH_OPS = PIECE_OPS[-1]


def third_plan(chained, experted):
    out, k = [], 0
    for item, n in zip(CHAIN, PIECES_AFTER):
        out += [("chain", item)] * chained
        for _ in range(n * experted):
            out.append(("experts", k))
            k += 1
    return out


def third_part(run, fori):
    run(0, 0, True, False)
    run(1, 1, True, True)
    run(2, 0, True, True)
    with fori(1, B // 2 - 1) as g:
        run(2 * g + 1, 1, True, True)
        run(2 * g + 2, 0, True, True)
    run(B - 1, (B - 1) % 2, True, True)
    run(B, B % 2, False, True)


def build(nc, x, L0_tok_W, L0_tok_b, L0_attn_W_v, L0_attn_W_theta, L0_ffn_w_gating, L0_ffn_gamma,
          L0_ffn_w1, L0_ffn_w2, L1_attn_Wq1, L1_attn_Wk1, L1_attn_Wq2, L1_attn_Wk2, L1_attn_Wv,
          L1_attn_Wo, L1_attn_gw1, L1_attn_gb1, L1_attn_gw2, L1_attn_gb2, L1_attn_gw3,
          L1_attn_gb3, L1_ffn_switch_w, L1_ffn_switch_b, L1_ffn_expert_w, L1_ffn_expert_b, out):
    ctx = ExitStack()
    with ctx:
        def sb(name, shape, dt=F32):
            return ctx.enter_context(nc.sbuf_tensor(name, shape, dt))

        def sem(name):
            return ctx.enter_context(nc.semaphore(name))

        parts_dram = nc.dram_tensor("parts_dram", (B * H, 4, PARTS, HD, N_ALL), BF16).ap()

        max_dram = nc.dram_tensor("max_dram", (SLOTS, PARTS, NT, P), BF16).ap()

        ident = sb("ident", [P, P])
        before = sb("before", [P, P], BF16)
        ones_bf = sb("ones_bf", [P, P], BF16)
        minus_half = sb("minus_half", [P, 1])
        plus_half = sb("plus_half", [P, 1])
        pick = sb("pick", [P, R * VD])
        rank_desc = sb("rank_desc", [P, E1])
        arena = sb("arena", [P, STEPS * NT * (VD + NST)])
        hid = [arena[:, i * HC * N_ALL:(i + 1) * HC * N_ALL].rearrange("p (k n) -> p k n", k=HC) for i in range(2)]
        w1_at = 2 * HC * N_ALL
        w1 = arena[:, w1_at:w1_at + E0 * HID].rearrange("p (e h) -> p e h", e=E0)
        w2_at = w1_at + E0 * HID
        w2 = arena[:, w2_at:w2_at + E0 * HC * C].rearrange("p (e k d) -> p e k d", e=E0, k=HC)
        nat_at = w2_at + E0 * HC * C
        w_nat = arena[:, nat_at:nat_at + (TAPS + 2 + E1) * P].rearrange("p (n c) -> p n c", c=P)
        o_all = arena[:, 0:STEPS * NT * VD].rearrange("p (j v) -> p j v", j=STEPS)
        stat_all = arena[:, STEPS * NT * VD:].rearrange("p (j v) -> p j v", j=STEPS)
        w_t = sb("w_t", [P, TAPS + 2 + E1, P])
        sw_nat = sb("sw_nat", [E1, P])
        sw_t = sb("sw_t", [P, E1])
        conv_b = sb("conv_b", [P, C])
        w_gate = sb("w_gate", [P, E0])
        gamma = sb("gamma", [P, 1])
        w_qk = sb("w_qk", [P, 4, C])
        w_v = sb("w_v", [P, C])
        w_o = sb("w_o", [P, C])
        g1 = sb("g1", [H * 8, H * GH1])
        g2 = sb("g2", [P, H * GH2 // 2])
        g3 = sb("g3", [P, H])
        gb1 = sb("gb1", [P, 1])
        gb2 = sb("gb2", [P, 1])
        gb3 = sb("gb3", [P, 1])
        ngb3 = sb("ngb3", [P, 1])
        sw_b = sb("sw_b", [P, E1])
        ex_b = sb("ex_b", [E1, C])

        def conv_w(i):
            return w_t[:, i, :]

        wv0_t = w_t[:, TAPS, :]
        wth_t = w_t[:, TAPS + 1, :]

        xin = sb("xin", [P, WT, R * C])
        x_t = sb("x_t", [P, R, PITCH + 2])
        h_cur = sb("h_cur", [P, NT, C])
        bn = sb("bn", [P, NT, 6])
        mv = sb("mv", [P, NT, 2])
        var_eps = sb("var_eps", [P, NT])
        rstd = sb("rstd", [P, NT])
        x1 = sb("x1", [P, NT, C + 1])
        x1_t = sb("x1_t", [P, N_ALL])
        gram = sb("gram", [P, C])
        x_mean = sb("x_mean", [P, P])
        gram_v = sb("gram_v", [P, C])
        kv = sb("kv", [P, C])
        xr = sb("xr", [P, NT, C])
        xr_t = sb("xr_t", [P, N_ALL])
        xf = sb("xf", [P, NT, C])
        xf_t = sb("xf_t", [P, N_ALL])
        r_a = sb("r_a", [P, NT, E1])
        r_b = sb("r_b", [P, NT, E1])
        r_c = sb("r_c", [P, NT, E1])
        r_p = sb("r_p", [P, NT, E1])
        r_m = sb("r_m", [P, NT])
        r_n = sb("r_n", [P, NT])
        r_g = sb("r_g", [P, NT])
        comb_next = sb("comb_next", [P, NT, E0])
        comb = sb("comb", [P, NT, E0])
        h_acc = sb("h_acc", [P, NT, C])
        h_two = sb("h_two", [P, NT, C])
        x3 = sb("x3", [P, NT, C])
        x3_t = sb("x3_t", [P, N_ALL])
        parts = sb("parts", [P, 4, PARTS, N_ALL], BF16)
        rest = sb("rest", [P, N_ALL])
        h_all = sb("h_all", [P, B, NT * C])
        v_all = sb("v_all", [P, B, NT * H, VD])

        ps = ctx.enter_context(nc.psum_tensor("ps", [P, 8, 512], F32))

        def pair(k):
            return ps[:, 2 * k:2 * k + 2, 0:PITCH]

        def pair_tile(k, t):
            return ps[:, 2 * k + t // WT, (t % WT) * P:(t % WT + 1) * P]

        def as_pair(ap):
            if len(ap.shape) == 3:
                return ap.rearrange("p (r w) c -> p r (w c)", r=R)
            return ap.rearrange("p (r c) -> p r c", r=R)

        s = {}
        for name in ("front_w_loaded", "w_loaded", "xin_clear", "psum_clear", "gate_clear", "x_t_clear", "ones_ready",
                     "ident_ready", "ngb3_ready", "dve_passed", "act_passed", "pool_passed", "pe_passed", "nat_ps", "nat_sb", "x_loaded", "dve_step",
                     "pool_step", "var_ready", "rstd_ready",
                     "xt_ps", "xt_sb", "conv_ps", "x1_sb", "gram_ps", "gram_sb", "gram_v_ps", "gram_v_sb",
                     "kv_ps", "kv_sb", "x1t_ps", "x1t_sb", "attn_ps", "xr_sb", "xrt_ps", "xrt_sb",
                     "route_ps", "logit_sb", "exp_sb", "xf_sb", "xft_ps", "xft_sb", "comb_sb", "up_ps", "hid_sb",
                     "down_ps", "ffn_acc", "h2_sb", "h_stored", "x3_sb", "x3t_ps", "x3t_sb", "qk_ps",
                     "part1_sb", "qk_split", "v_ps", "v_sb", "p1_done",
                     "row_scored", "neg_max", "row_exp", "min_done", "max_parts", "max_turned", "max_stored",
                     "t_scored", "t_exp", "av_done", "ot_sb", "o_turned", "o_copied", "vh_ready", "stat_saved",
                     "feat_ready", "pow_in", "pow_out", "feat_ps", "feat_sb", "g1_ps", "g1_sb", "g2_ps",
                     "g2_sb", "g3_ps", "g3_sb", "fused", "fused_ps", "fused_sb", "wo_ps", "x4_sb", "x4t_ps",
                     "x4t_sb", "route1_ps", "logit1_sb", "exp1_sb", "onehot", "rank_ps", "mask_sb", "mask_ps", "maskt_sb",
                     "bias_ps", "ex_ps", "ex_added", "ex_weighed", "side_step", "side_ready", "y_stored"):
            s[name] = sem(name)
        parts_stored = [sem(f"parts_stored{i}") for i in range(4)]
        stack_loaded = [sem(f"stack_loaded{i}") for i in range(SLOTS)]
        shift_loaded = [sem(f"shift_loaded{i}") for i in range(SLOTS)]

        front_loads = [
            (w_nat[:, 0:TAPS, :], L0_tok_W.rearrange("o (i c) -> o i c", i=TAPS)),
            (w_nat[:, TAPS, :], L0_attn_W_v),
            (w_nat[:, TAPS + 1, :], L0_attn_W_theta),
            (conv_b[:, :], L0_tok_b.partition_broadcast(P)),
            (w_gate[:, :], L0_ffn_w_gating),
            (gamma[:, :], L0_ffn_gamma.rearrange("(d o) -> d o", o=1)),
        ]
        weight_loads = [
            (w_nat[:, TAPS + 2:, :], L1_ffn_expert_w.rearrange("e f d -> f e d")),
            (sw_nat[:, :], L1_ffn_switch_w),
            (w1[:, :, :], L0_ffn_w1.rearrange("e d h -> d e h")),
            (w_qk[:, 0, :], L1_attn_Wq1), (w_qk[:, 1, :], L1_attn_Wk1),
            (w_qk[:, 2, :], L1_attn_Wq2), (w_qk[:, 3, :], L1_attn_Wk2),
            (w_v[:, :], L1_attn_Wv), (w_o[:, :], L1_attn_Wo),
            (sw_b[:, :], L1_ffn_switch_b.partition_broadcast(P)),
            (ex_b[:, :], L1_ffn_expert_b),
            (gb3[:, :], L1_attn_gb3.partition_broadcast(P)),
        ]
        for e in range(E0):
            weight_loads.append((w2[:, e, :, :], L0_ffn_w2[e].rearrange("(k h) d -> h k d", k=HC)))
        for i in range(H):
            weight_loads.append((g1[8 * i:8 * i + 8, GH1 * i:GH1 * (i + 1)], L1_attn_gw1))
            weight_loads.append((g3[GH2 * i:GH2 * (i + 1), i:i + 1], L1_attn_gw3))
            weight_loads.append((gb2[GH2 * i:GH2 * (i + 1), :], L1_attn_gb2.rearrange("(d o) -> d o", o=1)))
        for i in range(H // 2):
            weight_loads.append((g2[GH1 * i:GH1 * (i + 1), GH2 * i:GH2 * (i + 1)], L1_attn_gw2))
            weight_loads.append((gb1[GH1 * i:GH1 * (i + 1), :], L1_attn_gb1.rearrange("(d o) -> d o", o=1)))
        N_WLOAD = 16 * len(weight_loads)

        stacks = parts[0:STACK, :, :, :].rearrange("p n a c -> p (n a) c")
        q_st = [stacks[:, i, :] for i in range(SLOTS)]
        k_st = [stacks[:, SLOTS + i, :] for i in range(SLOTS)]
        stat = [sb(f"stat{i}", [P, NST, NT]) for i in range(SLOTS)]
        mp = [sb(f"mp{i}", [P, 32], BF16) for i in range(2)]
        mp_r = sb("mp_r", [P, 2, NT])
        mp_t = [sb(f"mp_t{i}", [P, 32], BF16) for i in range(SLOTS)]
        f_ring = [a[:, 0:R * W].rearrange("p (r w) -> p r w", r=R) for a in (
            xin[:, :, :].rearrange("p a c -> p (a c)"), rest, x_t[:, :, :].rearrange("p r w -> p (r w)"),
            x1[:, :, :].rearrange("p t c -> p (t c)"))]
        e_ring = [as_pair(a[:, :]) for a in (x1_t, xr_t, xf_t, x3_t)]
        o_t = [h_cur[:, :, :].rearrange("p t c -> p (t c)")[:, i * PITCH:i * PITCH + W] for i in range(2)]
        v_head = [sb(f"v_head{i}", [P, NT, VD]) for i in range(2)]

        h3, x4, fo_t = h_cur, xr, xf_t
        y = [h_acc, h_two]
        x4_t = [xr_t, x3_t]
        flat = [xin[:, :, :].rearrange("p a c -> p (a c)"), rest, x_t[:, :, :].rearrange("p r w -> p (r w)"),
                x1[:, :, :].rearrange("p t c -> p (t c)")]
        weighed = [[a[:, 0:4 * C] for a in flat[0:2]], [a[:, 0:4 * C] for a in flat[2:4]]]
        side = [flat[0][:, 4 * C:6 * C], flat[1][:, 4 * C:6 * C]]
        inv_s = sb("inv_s", [P, H * 2, NT])
        sum_p = sb("sum_p", [P, H * 2, NT])
        sq_p = sb("sq_p", [P, H * 2, NT])
        pw_in = sb("pw_in", [P, H * 2 * NT])
        pw_out = sb("pw_out", [P, H * 2 * NT])
        low_p = sb("low_p", [P, H * 2, NT])
        feat = sb("feat", [P, WT, H, 2, 4])
        feat_t = sb("feat_t", [H * 8, PITCH])
        hid1 = x1_t[:, :].rearrange("p (a w) -> p a w", a=2)
        hid2 = sb("hid2", [P, PITCH])
        alpha = sb("alpha", [P, WT, H])
        beta = sb("beta", [P, WT, H])
        coef = sb("coef", [P, 2, H, NT])
        fo = [a[:, :, :].rearrange("p t (h d) -> p t h d", h=H) for a in (xf, x3)]
        oh = sb("oh", [P, NT, E1])
        ohs = sb("ohs", [P, WT, E1], BF16)
        carry = sb("carry", [P, E1])
        mask = [sb(f"mask{i}", [P, NT, E1]) for i in range(2)]
        mask_t = sb("mask_t", [E1, N_ALL])
        self_c = sb("self_c", [P, NT])

        N_NAT = TAPS + 2 + E1
        FRONT_NAT = TAPS + 2
        x_view = x.rearrange("b (w r) c -> b w (r c)", r=R)
        out_view = out.rearrange("b (w r) c -> b w r c", r=R)

        block = ctx.enter_context(nc.Block())

        def is_alone(i):
            return isinstance(i, int) and i == B + 1

        def qk_pair(n, alone):
            return n if alone else 0

        def first_part(run):
            fill = plan(True, False, False)
            fill.insert(fill.index(("front", "attn")) + 1, ("front", "turn_weights"))
            run(0, fill)
            run(1, plan(True, True, False))
            return plan(True, True, True)

        @block.sync
        def _(sp):
            for dst, src in front_loads:
                sp.dma_start(dst, src).then_inc(s["front_w_loaded"], 16)

            def load_x(b):
                need(sp, s["xt_ps"], b)
                sp.dma_start(xin[:, 0:2, :], x_view[b, 0:2 * P, :].rearrange("(a p) c -> p a c", p=P)).then_inc(s["x_loaded"], 16)
                sp.dma_start(xin[0:W_IN - 2 * P, 2, :], x_view[b, 2 * P:W_IN, :]).then_inc(s["x_loaded"], 16)

            def store_parts(b):
                for n in range(4):
                    need(sp, s["qk_split"], 4 * b + n + 1)
                    for h in range(H):
                        sp.dma_start(parts_dram[b * H + h, n].rearrange("a d c -> d a c"),
                                     parts[h * HD:(h + 1) * HD, n, :, :]).then_inc(parts_stored[n], 16)

            sp.wait_ge(s["xin_clear"], 1)
            load_x(0)
            sp.wait_ge(s["gate_clear"], 1)
            for dst, src in weight_loads:
                sp.dma_start(dst, src).then_inc(s["w_loaded"], 16)
            load_x(1)
            with sp.Fori(2, B) as i:
                load_x(i)
                store_parts(i - 2)
            store_parts(B - 2)
            store_parts(B - 1)
            for n in range(4):
                sp.wait_ge(parts_stored[n], 16 * H * B)

            def load_stacks(bh, m, slot, j):
                need(sp, s["t_scored"], NT * (j - SLOTS + 1))
                q, k = parts_dram[bh, 2 * m], parts_dram[bh, 2 * m + 1]
                row = 0
                for p in range(PARTS):
                    n = (PARTS - p) * HD
                    sp.dma_start(q_st[slot][row:row + n, :],
                                 q[0:PARTS - p].rearrange("a d c -> (a d) c")).then_inc(stack_loaded[slot], 16)
                    for a in range(PARTS - p):
                        sp.dma_start(k_st[slot][row + a * HD:row + (a + 1) * HD, :],
                                     k[p]).then_inc(stack_loaded[slot], 16)
                    row += n

            def load_shift(slot, j):
                need(sp, s["max_turned"], j + 1)
                for q in range(4):
                    sp.dma_start(max_dram[slot].rearrange("a t w -> (a t) w")[:, 32 * q:32 * q + 32],
                                 mp_t[slot][32 * q:32 * q + PARTS * NT, :]).then_inc(s["max_stored"], 16)
                sp.wait_ge(s["max_stored"], 64 * (j + 1))
                sp.dma_start(q_st[slot][SHIFT0:STACK, :],
                             max_dram[slot].rearrange("a t w -> a (t w)")).then_inc(shift_loaded[slot], 16)

            def steps(g, last):
                for slot in range(SLOTS):
                    j = g * SLOTS + slot
                    load_shift(slot, j)
                    nxt = slot + SLOTS - 1
                    if nxt >= SLOTS and last:
                        continue
                    load_stacks(g * 2 + nxt // 2, nxt % 2, nxt % SLOTS, j + SLOTS - 1)

            for j in range(SLOTS - 1):
                load_stacks(j // 2, j % 2, j, j)
            steps(0, False)
            with sp.Fori(1, BODIES - 1) as g:
                steps(g, False)
            steps(BODIES - 1, True)

            def store_y(b, parity):
                sp.wait_ge(s["ex_added"], BATCH_OPS * (b + 1))
                for wt in range(WT):
                    n = ROWS[wt]
                    sp.dma_start(out_view[b, wt * P:wt * P + n, :, :],
                                 y[parity][0:n, wt:NT:WT, :]).then_inc(s["y_stored"], 16)

            with sp.Fori(0, B // 2) as g:
                store_y(2 * g, 0)
                store_y(2 * g + 1, 1)
            sp.wait_ge(s["y_stored"], 16 * WT * B)

        @block.tensor
        def _(pe):
            def turn(k, src):
                for t in range(NT):
                    last = nc.tensor.transpose(pair_tile(k, t), src[:, t, 0:C], ident[:, :])
                return last

            def per_tile(k, stationary, moving):
                for t in range(NT):
                    for n, (lhs, rhs) in enumerate(zip(stationary, moving)):
                        last = nc.tensor.matmul(pair_tile(k, t), lhs(t), rhs, start=(n == 0), stop=(n == len(moving) - 1))
                return last

            pe.wait_ge(s["front_w_loaded"], 16 * len(front_loads))
            pe.wait_ge(s["psum_clear"], 1)
            pe.wait_ge(s["ident_ready"], 1)
            for n in range(FRONT_NAT):
                nc.tensor.transpose(ps[:, n, 0:P], w_nat[:, n, :], ident[:, :]).then_inc(s["nat_ps"], 1)
            pe.wait_ge(s["nat_sb"], FRONT_NAT)

            def cols(buf):
                return lambda t: buf[:, tile_cols(t):tile_cols(t) + P]

            def front(item, b):
                if item == "turn_weights":
                    pe.wait_ge(s["w_loaded"], N_WLOAD)
                    for n in range(FRONT_NAT, N_NAT + 1):
                        need(pe, s["nat_sb"], n - 3 if n >= FRONT_NAT + 4 else 0)
                        if n < N_NAT:
                            nc.tensor.transpose(ps[:, 2 + n % 4, 0:P], w_nat[:, n, :], ident[:, :]).then_inc(s["nat_ps"], 1)
                        else:
                            nc.tensor.transpose(ps[:, 2 + n % 4, 0:E1], sw_nat[:, :], ident[0:E1, 0:E1]).then_inc(s["nat_ps"], 1)
                    pe.wait_ge(s["nat_sb"], N_NAT + 1)
                elif item == "xt":
                    need(pe, s["x_loaded"], 32 * (b + 1))
                    need(pe, s["xft_sb"], b)
                    need(pe, s["v_sb"], b - 1)
                    for wt in range(WT):
                        for r in range(R):
                            last = nc.tensor.transpose(pair_tile(0, r * WT + wt), xin[:, wt, r * C:(r + 1) * C], ident[:, :])
                    last.then_inc(s["xt_ps"], 1)
                elif item == "conv":
                    pe.wait_ge(s["xt_sb"], b + 1)
                    for t in range(NT):
                        r, w0 = t // WT, (t % WT) * P
                        for i in range(TAPS):
                            c0 = w0 + (r + i) // R
                            last = nc.tensor.matmul(pair_tile(0, t), x_t[:, (r + i) % R, c0:c0 + P], conv_w(i),
                                                    start=(i == 0), stop=(i == TAPS - 1))
                    last.then_inc(s["conv_ps"], 1)
                elif item == "gram":
                    pe.wait_ge(s["x1_sb"], b + 1)
                    for t in range(NT):
                        last = nc.tensor.matmul(ps[:, 0, 0:C + 1], x1[0:ROWS[t], t, 0:C], x1[0:ROWS[t], t, :],
                                                start=(t == 0), stop=(t == NT - 1))
                    last.then_inc(s["gram_ps"], 1)
                elif item == "gram_v":
                    pe.wait_ge(s["gram_sb"], b + 1)
                    nc.tensor.matmul(ps[:, 1, 0:C], gram[:, :], wv0_t, start=True, stop=True).then_inc(s["gram_v_ps"], 1)
                elif item == "kv":
                    pe.wait_ge(s["gram_v_sb"], b + 1)
                    nc.tensor.matmul(ps[:, 0, 0:C], wth_t, gram_v[:, :], start=True, stop=True).then_inc(s["kv_ps"], 1)
                elif item == "x1t":
                    pe.wait_ge(s["kv_sb"], b + 1)
                    turn(0, x1).then_inc(s["x1t_ps"], 1)
                elif item == "attn":
                    pe.wait_ge(s["x1t_sb"], b + 1)
                    per_tile(0, [cols(x1_t), lambda t: x_mean[:, :]], [kv[:, :], wv0_t]).then_inc(s["attn_ps"], 1)
                elif item == "xrt":
                    pe.wait_ge(s["xr_sb"], b + 1)
                    turn(0, xr).then_inc(s["xrt_ps"], 1)
                elif item == "route":
                    pe.wait_ge(s["xrt_sb"], b + 1)
                    for t in range(NT):
                        last = nc.tensor.matmul(ps[:, 0, t * E0:(t + 1) * E0], cols(xr_t)(t), w_gate[:, :],
                                                start=(t == 0), stop=(t == NT - 1), skip_group_check=True)
                    last.then_inc(s["route_ps"], 1)
                elif item == "xft":
                    pe.wait_ge(s["logit_sb"], b + 1)
                    pe.wait_ge(s["xf_sb"], b + 1)
                    turn(0, xf).then_inc(s["xft_ps"], 1)

            def ffn(item, b):
                if item[0] == "up":
                    _, e, k = item
                    n = (HC * E0) * b + HC * e + k
                    if e == 0 and k == 0:
                        pe.wait_ge(s["xft_sb"], b + 1)
                    need(pe, s["hid_sb"], n - 1)
                    for r in range(R):
                        last = nc.tensor.matmul(ps[:, 2 + 2 * (k % 2) + r, 0:PITCH], w1[:, e, k * P:(k + 1) * P],
                                                xf_t[:, r * PITCH:(r + 1) * PITCH], start=True, stop=True)
                    last.then_inc(s["up_ps"], 1)
                elif item[0] == "down":
                    _, e, t = item
                    if t == 0:
                        pe.wait_ge(s["hid_sb"], HC * (E0 * b + e + 1))
                        need(pe, s["ffn_acc"], E0 * b + e)
                    for k in range(HC):
                        last = nc.tensor.matmul(pair_tile(3, t), hid[e % 2][:, k, tile_cols(t):tile_cols(t) + P],
                                                w2[:, e, k, :], start=(k == 0), stop=(k == HC - 1))
                    if t == NT - 1:
                        last.then_inc(s["down_ps"], 1)

            def back(item, b, pair_reader, alone=False):
                if item == "x3t":
                    pe.wait_ge(s["x3_sb"], b + 1)
                    need(pe, s["xft_sb"], pair_reader)
                    turn(0, x3).then_inc(s["x3t_ps"], 1)
                elif item == "x3n":
                    pass
                elif item == "v":
                    need(pe, s["qk_split"], 4 * b + 4)
                    per_tile(0, [cols(x3_t)], [w_v[:, :]]).then_inc(s["v_ps"], 1)
                else:
                    n = int(item[2])
                    pe.wait_ge(s["x3t_sb"], b + 1)
                    if n and not alone:
                        pe.wait_ge(s["qk_split"], 4 * b + n)
                    for r in range(R):
                        last = nc.tensor.matmul(ps[:, 2 * qk_pair(n, alone) + r, 0:PITCH], w_qk[:, n, :], x3_t[:, r * PITCH:(r + 1) * PITCH],
                                                start=True, stop=True)
                    last.then_inc(s["qk_ps"], 1)

            def run(i, items):
                for kind, item in items:
                    if kind == "front":
                        front(item, i)
                    elif kind == "ffn":
                        ffn(item, i - 1)
                    else:
                        back(item, i - 2, i if not isinstance(i, int) or i < B else B, is_alone(i))

            both = first_part(run)
            with pe.Fori(2, B) as i:
                run(i, both)
            run(B, plan(False, True, True))
            run(B + 1, plan(False, False, True))

            def row_scores(g, slot, t):
                j = g * SLOTS + slot
                if t == 0:
                    pe.wait_ge(stack_loaded[slot], 16 * 9 * (g + 1))
                n = NT * j + t
                need(pe, s["row_exp"], n - 1)
                m, c0 = ROWS[t], tile_cols(t)
                for r in range(R):
                    last = nc.tensor.matmul(ps[0:m, 2 * (t % 2) + r, 0:W], q_st[slot][0:SK, c0:c0 + m],
                                            k_st[slot][0:SK, r * PITCH:r * PITCH + W], start=True, stop=True)
                last.then_inc(s["row_scored"], 1)

            def turned_scores(g, slot, t):
                j = g * SLOTS + slot
                if t == 0:
                    pe.wait_ge(shift_loaded[slot], 16 * (g + 1))
                n = NT * j + t
                need(pe, s["t_exp"], n)
                m, c0 = ROWS[t], tile_cols(t)
                for r in range(R):
                    last = nc.tensor.matmul(ps[0:m, 4 + r, 0:W], k_st[slot][0:STACK, c0:c0 + m],
                                            q_st[slot][0:STACK, r * PITCH:r * PITCH + W], start=True, stop=True)
                last.then_inc(s["t_scored"], 1)

            def weighted_values(g, slot, kt):
                j = g * SLOTS + slot
                n = NT * j + kt
                bank = 6 + slot % 2
                if kt == 0:
                    if slot % 2 == 0:
                        pe.wait_ge(s["vh_ready"], 2 * g + slot // 2 + 1)
                    need(pe, s["o_copied"], j - 1)
                pe.wait_ge(s["t_exp"], n + 2)
                for k in (kt, kt + 1):
                    m = ROWS[k]
                    for r in range(R):
                        c = 32 * (R * (k % 2) + r)
                        last = nc.tensor.matmul(ps[c:c + VD, bank, 0:W], v_head[slot // 2][0:m, k, :],
                                                e_ring[n_slot(slot, k)][0:m, r, 0:W], start=(kt == 0), stop=(kt == NT - 2))
                last.then_inc(s["av_done"], 2)

            def turn_o(g, slot):
                pe.wait_ge(s["ot_sb"], g * SLOTS + slot + 1)
                for wt in range(WT):
                    q = ROWS[wt]
                    last = nc.tensor.matmul(ps[0:q, 6 + slot % 2, PITCH + wt * R * VD:PITCH + (wt + 1) * R * VD],
                                            o_t[slot % 2][0:OT_ROWS, wt * P:wt * P + q], pick[0:OT_ROWS, :],
                                            start=(wt == 0), stop=True, skip_group_check=True)
                last.then_inc(s["o_turned"], 1)

            def behind(g, n, first=False):
                n -= PE_LAG
                if first and n < 0:
                    return
                g, slot = (g, n // NT) if n >= 0 else (g - 1, n // NT + SLOTS)
                t = n % NT
                turned_scores(g, slot, t)
                very_first = first and slot == 0
                if t in (2, 4):
                    weighted_values(g, slot, t - 2)
                elif t == 0 and not very_first:
                    weighted_values(*earlier(g, slot, 1), NT - 2)
                elif t == 3 and not very_first:
                    turn_o(*earlier(g, slot, 1))

            pe.wait_ge(s["p1_done"], 1)
            for n in range(SLOTS * NT):
                row_scores(0, n // NT, n % NT)
                behind(0, n, True)
            with pe.Fori(1, BODIES) as g:
                for n in range(SLOTS * NT):
                    row_scores(g, n // NT, n % NT)
                    behind(g, n)
            for n in range(PE_LAG):
                behind(BODIES, n)
            weighted_values(BODIES - 1, SLOTS - 1, NT - 2)
            turn_o(BODIES - 1, SLOTS - 1)

            def chain(item, b, parity):
                if item == "feat":
                    pe.wait_ge(s["feat_ready"], b + 1)
                    settle(pe, s["pe_passed"])
                    for wt in range(WT):
                        last = nc.tensor.transpose(ps[0:H * 8, 0, wt * P:(wt + 1) * P],
                                                   feat[:, wt].rearrange("p h m f -> p (h m f)"), ident[:, :])
                    last.then_inc(s["feat_ps"], 1)
                elif item == "g1":
                    pe.wait_ge(s["feat_sb"], b + 1)
                    for i in range(2):
                        last = nc.tensor.matmul(ps[:, 2 + i, 0:PITCH], g1[:, i * P:(i + 1) * P], feat_t[:, :], start=True, stop=True)
                    last.then_inc(s["g1_ps"], 1)
                elif item == "g2":
                    pe.wait_ge(s["g1_sb"], b + 1)
                    for i in range(2):
                        last = nc.tensor.matmul(ps[64 * i:64 * i + 64, 0, 0:PITCH], g2[:, :], hid1[:, i, :], start=True, stop=True)
                    last.then_inc(s["g2_ps"], 1)
                elif item == "g3":
                    pe.wait_ge(s["g2_sb"], b + 1)
                    for wt in range(WT):
                        last = nc.tensor.matmul(ps[:, 2, wt * H:(wt + 1) * H], hid2[:, wt * P:(wt + 1) * P], g3[:, :],
                                                start=(wt == 0), stop=(wt == WT - 1), skip_group_check=True)
                    last.then_inc(s["g3_ps"], 1)
                elif item == "fuse":
                    pe.wait_ge(s["fused"], b + 1)
                    for t in range(NT):
                        last = nc.tensor.transpose(pair_tile(0, t), fo[0][:, t].rearrange("p h d -> p (h d)"), ident[:, :])
                    last.then_inc(s["fused_ps"], 1)
                elif item == "wo":
                    pe.wait_ge(s["fused_sb"], b + 1)
                    per_tile(1, [cols(fo_t)], [w_o[:, :]]).then_inc(s["wo_ps"], 1)
                elif item == "x4":
                    pe.wait_ge(s["x4_sb"], b + 1)
                    turn(0, x4).then_inc(s["x4t_ps"], 1)
                elif item == "route":
                    pe.wait_ge(s["x4t_sb"], b + 1)
                    for t in range(NT):
                        last = nc.tensor.matmul(ps[:, 2, t * E1:(t + 1) * E1], cols(x4_t[parity])(t), sw_t[:, :],
                                                start=(t == 0), stop=(t == NT - 1), skip_group_check=True)
                    last.then_inc(s["route1_ps"], 1)
                elif item == "pick":
                    pe.wait_ge(s["onehot"], b + 1)
                    for wt in range(WT + 1):
                        for u in range(min(wt + 1, WT)):
                            m = ROWS[u]
                            last = nc.tensor.matmul(ps[:, 3, wt * E1:(wt + 1) * E1],
                                                    (before if u == wt else ones_bf)[0:m, :], ohs[0:m, u, :],
                                                    start=(wt == 0 and u == 0), stop=(u == min(wt, WT - 1)), skip_group_check=True)
                    last.then_inc(s["rank_ps"], 1)
                elif item == "mask":
                    pe.wait_ge(s["mask_sb"], b + 1)
                    settle(pe, s["pe_passed"])
                    for t in range(NT):
                        last = nc.tensor.transpose(ps[0:E1, t // WT, (t % WT) * P:(t % WT + 1) * P], mask[parity][:, t, :], ident[:, :])
                    last.then_inc(s["mask_ps"], 1)
                elif item == "bias":
                    pe.wait_ge(s["maskt_sb"], b + 1)
                    for t in range(NT):
                        last = nc.tensor.matmul(pair_tile(1, t), mask_t[:, tile_cols(t):tile_cols(t) + P], ex_b[:, :],
                                                start=True, stop=True)
                    last.then_inc(s["bias_ps"], 1)

            def experts(k, b, parity):
                if k - 2 in SHARED:
                    pe.wait_ge(s["ex_weighed"], len(SHARED) * b + SHARED.index(k - 2) + 1)
                elif k >= 2:
                    pe.wait_ge(s["ex_added"], BATCH_OPS * b + PIECE_OPS[k - 2])
                else:
                    need(pe, s["ex_added"], BATCH_OPS * (b - 1) + PIECE_OPS[PIECES + k - 2])
                for t, q, bank in piece(k):
                    nc.tensor.matmul(ps[:, bank, :], cols(x4_t[parity])(t),
                                     w_t[:, TAPS + 2 + 4 * q:TAPS + 6 + 4 * q, :].rearrange("p a b -> p (a b)"),
                                     start=True, stop=True).then_inc(s["ex_ps"], 1)

            def run(i, parity, chained, experted):
                if experted:
                    for k in range(LEAD):
                        experts(k, i - 1, 1 - parity)
                for kind, item in third_plan(chained, experted):
                    if kind == "chain":
                        chain(item, i, parity)
                    elif item + LEAD < PIECES:
                        experts(item + LEAD, i - 1, 1 - parity)

            third_part(run, pe.Fori)

        @block.scalar
        def _(act):
            def copy(dst, src, name, scale=1.0):
                nc.scalar.activation(dst, src, ACT.Copy, scale=scale).then_inc(s[name], 1)

            for n in range(FRONT_NAT):
                act.wait_ge(s["nat_ps"], n + 1)
                copy(w_t[:, n, :], ps[:, n, 0:P], "nat_sb")

            def front(item, b):
                if item == "turn_weights":
                    for n in range(FRONT_NAT, N_NAT + 1):
                        act.wait_ge(s["nat_ps"], n + 1)
                        if n < N_NAT:
                            copy(w_t[:, n, :], ps[:, 2 + n % 4, 0:P], "nat_sb")
                        else:
                            copy(sw_t[:, :], ps[:, 2 + n % 4, 0:E1], "nat_sb")
                elif item == "xt":
                    act.wait_ge(s["xt_ps"], b + 1)
                    if isinstance(b, int) and b == 0:
                        act.wait_ge(s["x_t_clear"], 1)
                    need(act, s["conv_ps"], b)
                    copy(x_t[:, :, 0:PITCH], pair(0), "xt_sb")
                elif item == "gram":
                    act.wait_ge(s["gram_ps"], b + 1)
                    need(act, s["attn_ps"], b)
                    nc.scalar.activation(gram[:, :], ps[:, 0, 0:C], ACT.Copy)
                    copy(x_mean[:, :], ps[:, 0, C:C + 1].to_broadcast((P, P)), "gram_sb", 1.0 / L)
                elif item == "gram_v":
                    act.wait_ge(s["gram_v_ps"], b + 1)
                    copy(gram_v[:, :], ps[:, 1, 0:C], "gram_v_sb")
                elif item == "kv":
                    act.wait_ge(s["kv_ps"], b + 1)
                    copy(kv[:, :], ps[:, 0, 0:C], "kv_sb", 1.0 / (L * C ** 0.5))
                elif item == "x1t":
                    act.wait_ge(s["x1t_ps"], b + 1)
                    copy(as_pair(x1_t[:, :]), pair(0), "x1t_sb")
                elif item == "xrt":
                    act.wait_ge(s["xrt_ps"], b + 1)
                    need(act, s["route_ps"], b)
                    copy(as_pair(xr_t[:, :]), pair(0), "xrt_sb")
                elif item == "route":
                    act.wait_ge(s["logit_sb"], b + 1)
                    nc.scalar.activation(r_b[:, :, 0:E0], r_a[:, :, 0:E0], ACT.Exp).then_inc(s["exp_sb"], 1)
                elif item == "xft":
                    act.wait_ge(s["xft_ps"], b + 1)
                    need(act, s["up_ps"], HC * E0 * b)
                    copy(as_pair(xf_t[:, :]), pair(0), "xft_sb", gamma[:, 0:1])

            def ffn(item, b):
                if item[0] == "up":
                    _, e, k = item
                    n = (HC * E0) * b + HC * e + k
                    act.wait_ge(s["up_ps"], n + 1)
                    if k == 0:
                        need(act, s["down_ps"], E0 * b + e - 1)
                    nc.scalar.activation(as_pair(hid[e % 2][:, k, :]), pair(1 + k % 2), ACT.Gelu).then_inc(s["hid_sb"], 1)

            def back(item, b, alone):
                if item == "x3t":
                    act.wait_ge(s["x3t_ps"], b + 1)
                    need(act, s["v_ps"], b)
                    copy(as_pair(x3_t[:, :]), pair(0), "x3t_sb")
                elif item not in ("v", "x3n"):
                    n = int(item[2])
                    act.wait_ge(s["qk_ps"], 4 * b + n + 1)
                    need(act, parts_stored[n], 16 * H * b)
                    copy(as_pair(parts[:, n, 0, :]), pair(qk_pair(n, alone)), "part1_sb", 2.0 * HD ** -0.5 if n % 2 == 0 else 1.0)

            def run(i, items):
                for kind, item in items:
                    if kind == "front":
                        front(item, i)
                    elif kind == "ffn":
                        ffn(item, i - 1)
                    else:
                        back(item, i - 2, is_alone(i))

            both = first_part(run)
            with act.Fori(2, B) as i:
                run(i, both)
            run(B, plan(False, True, True))
            run(B + 1, plan(False, False, True))

            def row_exp(j, slot, t):
                n = NT * j + t
                act.wait_ge(s["neg_max"], n + 1)
                need(act, s["min_done"], n - 3)
                if t == 0:
                    need(act, s["stat_saved"], j - SLOTS + 1)
                nc.scalar.activation(f_ring[(NT * slot + t) % 4][:, :, :], ps[:, 2 * (t % 2):2 * (t % 2) + 2, 0:W], ACT.Exp,
                                     bias=stat[slot][:, 0, t:t + 1],
                                     accum_out=stat[slot][:, 1, t:t + 1]).then_inc(s["row_exp"], 1)

            def turned_exp(j, slot, t):
                n = NT * j + t
                act.wait_ge(s["t_scored"], n + 1)
                need(act, s["av_done"], n - ERING + 1)
                nc.scalar.activation(e_ring[n_slot(slot, t)][:, :, 0:W], ps[:, 4:6, 0:W], ACT.Exp,
                                     scale=0.5).then_inc(s["t_exp"], 1)

            def copy_ot(j, slot):
                act.wait_ge(s["av_done"], NT * (j + 1))
                nc.scalar.activation(o_t[slot % 2][0:OT_ROWS, :], ps[0:OT_ROWS, 6 + slot % 2, 0:W], ACT.Copy).then_inc(s["ot_sb"], 1)

            def save_o(j, slot):
                act.wait_ge(s["o_turned"], j + 1)
                settle(act, s["act_passed"])
                nc.scalar.activation(o_all[:, bass.ds(j, 1), :].rearrange("p a (r w v) -> p (a r) w v", r=R, w=WT),
                                     ps[:, 6 + slot % 2, PITCH:PITCH + NT * VD].rearrange("p (w r v) -> p r w v", r=R, w=WT),
                                     ACT.Copy).then_inc(s["o_copied"], 1)

            def steps(g, first):
                for slot in range(SLOTS):
                    j = g * SLOTS + slot
                    for t in range(NT):
                        row_exp(j, slot, t)
                        if not (first and slot <= LAG):
                            if t == 1:
                                copy_ot(j - LAG - 1, (slot - LAG - 1) % SLOTS)
                            elif t == 5:
                                save_o(j - LAG - 1, (slot - LAG - 1) % SLOTS)
                        if not (first and slot < LAG):
                            turned_exp(j - LAG, (slot - LAG) % SLOTS, t)

            steps(0, True)
            with act.Fori(1, BODIES) as g:
                steps(g, False)
            for j in range(STEPS - LAG, STEPS):
                for t in range(NT):
                    turned_exp(j, j % SLOTS, t)
                    if t == 1:
                        copy_ot(j - 1, (j - 1) % SLOTS)
                    elif t == 5:
                        save_o(j - 1, (j - 1) % SLOTS)
            copy_ot(STEPS - 1, SLOTS - 1)
            save_o(STEPS - 1, SLOTS - 1)

            def chain(item, b, parity):
                if item == "feat":
                    act.wait_ge(s["feat_ps"], b + 1)
                    copy(feat_t[:, :], ps[0:H * 8, 0, 0:PITCH], "feat_sb")
                elif item == "g1":
                    act.wait_ge(s["g1_ps"], b + 1)
                    nc.scalar.activation(hid1[:, :, :], ps[:, 2:4, 0:PITCH], ACT.Relu, bias=gb1[:, 0:1]).then_inc(s["g1_sb"], 1)
                elif item == "g2":
                    act.wait_ge(s["g2_ps"], b + 1)
                    nc.scalar.activation(hid2[:, :], ps[:, 0, 0:PITCH], ACT.Relu, bias=gb2[:, 0:1]).then_inc(s["g2_sb"], 1)
                elif item == "g3":
                    act.wait_ge(s["g3_ps"], b + 1)
                    nc.scalar.activation(alpha[:, :, :].rearrange("p w h -> p (w h)"), ps[:, 2, 0:WT * H], ACT.Exp,
                                         scale=-1.0, bias=ngb3[:, 0:1]).then_inc(s["g3_sb"], 1)
                elif item == "fuse":
                    act.wait_ge(s["fused_ps"], b + 1)
                    copy(as_pair(fo_t[:, :]), pair(0), "fused_sb")
                elif item == "x4":
                    act.wait_ge(s["x4t_ps"], b + 1)
                    need(act, s["ex_ps"], 4 * NT * (b - 1))
                    copy(as_pair(x4_t[parity][:, :]), pair(0), "x4t_sb")
                elif item == "route":
                    act.wait_ge(s["logit1_sb"], b + 1)
                    nc.scalar.activation(r_b[:, :, :], r_a[:, :, :], ACT.Exp).then_inc(s["exp1_sb"], 1)
                elif item == "mask":
                    act.wait_ge(s["mask_ps"], b + 1)
                    copy(as_pair(mask_t[:, :]), ps[0:E1, 0:2, 0:PITCH], "maskt_sb")

            def experts(k, b, parity):
                if k not in SHARED:
                    return
                m = SHARED.index(k)
                need(act, s["side_ready"], len(SHARED) * b + m - 1)
                for i, (t, q, bank) in enumerate(piece(k)):
                    act.wait_ge(s["ex_ps"], 4 * NT * b + 2 * k + i + 1)
                    for e in range(4):
                        last = nc.scalar.activation(weighed[m % 2][i][:, e * C:(e + 1) * C], ps[:, bank, e * C:(e + 1) * C],
                                                    ACT.Copy, scale=mask[parity][:, t, 4 * q + e:4 * q + e + 1])
                last.then_inc(s["ex_weighed"], 1)

            def run(i, parity, chained, experted):
                for kind, item in third_plan(chained, experted):
                    if kind == "chain":
                        chain(item, i, parity)
                    else:
                        experts(item, i - 1, 1 - parity)

            act.wait_ge(s["ngb3_ready"], 1)
            third_part(run, act.Fori)

        @block.gpsimd
        def _(pool):
            nc.gpsimd.memset(ident[:, :], 0.0).then_inc(s["pool_step"], 1)
            nc.gpsimd.memset(before[:, :], 1.0).then_inc(s["pool_step"], 1)
            nc.gpsimd.memset(ones_bf[:, :], 1.0)
            nc.gpsimd.memset(minus_half[:, :], -0.5)
            nc.gpsimd.memset(plus_half[:, :], 0.5)
            for i in range(2):
                nc.gpsimd.memset(mp[i][:, :], 0.0)
            nc.gpsimd.iota(rank_desc[:, :], pattern=[[-1, E1]], base=E1, channel_multiplier=0,
                           allow_small_or_imprecise_dtypes=True)
            pool.wait_ge(s["pool_step"], 2)
            nc.gpsimd.affine_select(out=before[:, :], in_=before[:, :], compare_op=ALU.is_gt, fill=0.0,
                                    base=0, pattern=[[1, P]], channel_multiplier=-1).then_inc(s["pool_step"], 1)
            nc.gpsimd.affine_select(out=ident[:, :], in_=ident[:, :], compare_op=ALU.not_equal, fill=1.0,
                                    base=0, pattern=[[-1, P]], channel_multiplier=1).then_inc(s["pool_step"], 1)
            nc.gpsimd.memset(pick[:, :], 0.0).then_inc(s["pool_step"], 1)
            for c in range(2 * R):
                pool.wait_ge(s["pool_step"], 5 + c)
                half = pick[:, (c % R) * VD:(c % R + 1) * VD]
                nc.gpsimd.affine_select(out=half, in_=half, compare_op=ALU.not_equal, fill=1.0,
                                        base=-32 * c, pattern=[[-1, VD]], channel_multiplier=1).then_inc(s["pool_step"], 1)
            pool.wait_ge(s["pool_step"], 9)
            pool.sem_inc(s["ident_ready"], 1)

            def norm(n):
                pool.wait_ge(s["var_ready"], n + 1)
                nc.gpsimd.tensor_tensor(rstd[:, :], var_eps[:, :], minus_half[:, 0:1].to_broadcast((P, NT)),
                                        ALU.pow).then_inc(s["rstd_ready"], 1)

            def run(i, items):
                n = 0
                for kind, item in items:
                    if item in ("conv", "attn", "xrt", "x3n"):
                        norm(norm_base(i) + n)
                        n += 1
                    if item == ("end",):
                        pool.wait_ge(s["h2_sb"], i)
                        settle(pool, s["pool_passed"])
                        nc.gpsimd.tensor_copy(h_all[:, bass.ds(i - 1, 1), :].rearrange("p a c -> p (a c)"),
                                              h_two[:, :, :].rearrange("p t c -> p (t c)")).then_inc(s["h_stored"], 1)

            both = first_part(run)
            with pool.Fori(2, B) as i:
                run(i, both)
            run(B, plan(False, True, True))
            run(B + 1, plan(False, False, True))

            pool.wait_ge(s["w_loaded"], N_WLOAD)
            nc.gpsimd.tensor_scalar(ngb3[:, :], gb3[:, :], -1.0, 0.0, ALU.mult, ALU.add).then_inc(s["ngb3_ready"], 1)

            def steps(g, first):
                for slot in range(SLOTS):
                    j = g * SLOTS + slot
                    if slot % 2 == 0:
                        bh = 2 * g + slot // 2
                        need(pool, s["av_done"], 2 * NT * (bh - 1))
                        settle(pool, s["pool_passed"])
                        nc.gpsimd.tensor_copy(
                            v_head[slot // 2][:, :, :],
                            v_all[:, bass.ds(g // (H // 2), 1), :, :].rearrange("p a (t h) d -> p (a t) h d", h=H)
                            [:, :, bass.ds((g % (H // 2)) * 2 + slot // 2, 1), :].rearrange("p t a d -> p t (a d)")
                        ).then_inc(s["vh_ready"], 1)
                    pool.wait_ge(s["neg_max"], NT * (j + 1))
                    need(pool, s["max_turned"], j - 1)
                    a = mp[slot % 2]
                    settle(pool, s["pool_passed"])
                    base = 9 + 4 * j + (0 if first and slot == 0 else j - 1)
                    nc.gpsimd.tensor_copy(a[:, 0:NT], stat[slot][:, 0, :]).then_inc(s["pool_step"], 1)
                    pool.wait_ge(s["pool_step"], base + 1)
                    nc.gpsimd.tensor_tensor(mp_r[:, 0, :], stat[slot][:, 0, :], a[:, 0:NT], ALU.subtract).then_inc(s["pool_step"], 1)
                    pool.wait_ge(s["pool_step"], base + 2)
                    settle(pool, s["pool_passed"])
                    nc.gpsimd.tensor_copy(a[:, NT:2 * NT], mp_r[:, 0, :]).then_inc(s["pool_step"], 1)
                    pool.wait_ge(s["pool_step"], base + 3)
                    nc.gpsimd.tensor_tensor(mp_r[:, 1, :], mp_r[:, 0, :], a[:, NT:2 * NT], ALU.subtract).then_inc(s["pool_step"], 1)
                    pool.wait_ge(s["pool_step"], base + 4)
                    settle(pool, s["pool_passed"])
                    nc.gpsimd.tensor_copy(a[:, 2 * NT:3 * NT], mp_r[:, 1, :]).then_inc(s["max_parts"], 1)
                    pool.wait_ge(s["max_parts"], j + 1)
                    if not (first and slot == 0):
                        save_stat(j - 1, (slot - 1) % SLOTS, j + 1)

            def save_stat(j, slot, split):
                pool.wait_ge(s["row_exp"], NT * (j + 1))
                pool.wait_ge(s["min_done"], NT * (j + 1))
                low = stat[slot][:, 2, :]
                nc.gpsimd.tensor_tensor(low, low, plus_half[:, 0:1].to_broadcast((P, NT)), ALU.pow).then_inc(s["pool_step"], 1)
                pool.wait_ge(s["pool_step"], 9 + 4 * split + j + 1)
                settle(pool, s["pool_passed"])
                nc.gpsimd.tensor_copy(stat_all[:, bass.ds(j, 1), :].rearrange("p a c -> p (a c)"),
                                      stat[slot][:, :, :].rearrange("p a c -> p (a c)")).then_inc(s["stat_saved"], 1)

            steps(0, True)
            with pool.Fori(1, BODIES) as g:
                steps(g, False)
            save_stat(STEPS - 1, SLOTS - 1, STEPS)

            def std(b):
                pool.wait_ge(s["pow_in"], b + 1)
                nc.gpsimd.tensor_tensor(pw_out[:, :], pw_in[:, :], plus_half[:, 0:1].to_broadcast((P, H * 2 * NT)),
                                        ALU.pow).then_inc(s["pow_out"], 1)

            def experts(k, b):
                if k not in SHARED:
                    return
                m = SHARED.index(k)
                n = len(SHARED) * b + m
                pool.wait_ge(s["ex_weighed"], n + 1)
                for i in range(2):
                    a = weighed[m % 2][i]
                    nc.gpsimd.tensor_tensor(a[:, 0:2 * C], a[:, 0:2 * C], a[:, 2 * C:4 * C], ALU.add).then_inc(s["side_step"], 1)
                if m >= 2:
                    pool.wait_ge(s["ex_added"], BATCH_OPS * b + ADD_OPS[m - 2])
                else:
                    need(pool, s["ex_added"], BATCH_OPS * (b - 1) + ADD_OPS[m + 2])
                for i in range(2):
                    a = weighed[m % 2][i]
                    pool.wait_ge(s["side_step"], 2 * n + i + 1)
                    last = nc.gpsimd.tensor_tensor(side[m % 2][:, i * C:(i + 1) * C], a[:, 0:C], a[:, C:2 * C], ALU.add)
                last.then_inc(s["side_ready"], 1)

            def run(i, parity, chained, experted):
                for kind, item in third_plan(chained, experted):
                    if kind == "experts":
                        experts(item, i - 1)
                    elif item == "wo":
                        norm(NLN0 * B + i)
                    elif item == "stats" and not (isinstance(i, int) and i == B - 1):
                        std(i + 1)

            std(0)
            third_part(run, pool.Fori)

        @block.vector
        def _(dve):
            nc.vector.memset(xin[:, :, :], 0.0).then_inc(s["xin_clear"], 1)
            nc.vector.memset(ps[:, :, :], 0.0).then_inc(s["psum_clear"], 1)
            nc.vector.memset(g1[:, :], 0.0)
            nc.vector.memset(g2[:, :], 0.0)
            nc.vector.memset(g3[:, :], 0.0).then_inc(s["gate_clear"], 1)
            nc.vector.memset(x_t[:, :, :], 0.0).then_inc(s["x_t_clear"], 1)
            nc.vector.memset(x1[:, :, :], 1.0)
            nc.vector.memset(carry[:, :], 0.0)
            nc.vector.memset(v_all[:, :, :, :].rearrange("p a b c -> p (a b c)"), 1.0).then_inc(s["ones_ready"], 1)
            dve.wait_ge(s["ones_ready"], 1)

            def norm_stats(c, src):
                for t in range(NT):
                    last = nc.vector.bn_stats(bn[:, t, :], src[:, t, 0:C])
                c.link(last)
                settle(dve, s["dve_passed"])
                for t in range(NT):
                    last = nc.vector.bn_aggr(mv[:, t, :], bn[:, t, :])
                c.link(last)
                nc.vector.tensor_scalar(var_eps[:, :], mv[:, :, 1], LN_EPS, None, ALU.add).then_inc(s["var_ready"], 1)

            def normalise(n, src, dst, name):
                dve.wait_ge(s["rstd_ready"], n + 1)
                for t in range(NT):
                    last = nc.vector.tensor_scalar(dst[:, t, 0:C], src[:, t, 0:C], mv[:, t, 0:1], rstd[:, t:t + 1],
                                                   ALU.subtract, ALU.mult)
                last.then_inc(s[name], 1)

            def norm(c, n, src, dst, name):
                norm_stats(c, src)
                normalise(n, src, dst, name)

            def bc(ap, n):
                return ap.unsqueeze(2).to_broadcast((P, NT, n))

            def soft_before(c, sem_in, n):
                c.link(nc.vector.tensor_reduce(r_m[:, :], r_c[:, :, 0:n], X_AXIS, ALU.max))
                nc.vector.tensor_tensor(r_a[:, :, 0:n], r_c[:, :, 0:n], bc(r_m[:, :], n), ALU.subtract).then_inc(s[sem_in], 1)

            def soft_after(c, sem_out, value, n):
                dve.wait_ge(s[sem_out], value)
                c.link(nc.vector.tensor_reduce(r_n[:, :], r_b[:, :, 0:n], X_AXIS, ALU.add))
                c.link(nc.vector.reciprocal(r_g[:, :], r_n[:, :]))
                c.link(nc.vector.tensor_tensor(r_p[:, :, 0:n], r_b[:, :, 0:n], bc(r_g[:, :], n), ALU.mult))
                c.link(nc.vector.tensor_reduce(r_m[:, :], r_p[:, :, 0:n], X_AXIS, ALU.max))
                c.link(nc.vector.tensor_tensor(r_a[:, :, 0:n], r_p[:, :, 0:n], bc(r_m[:, :], n), ALU.is_equal))
                c.link(nc.vector.tensor_tensor(r_c[:, :, 0:n], r_a[:, :, 0:n],
                                               rank_desc[:, 0:n].unsqueeze(1).to_broadcast((P, NT, n)), ALU.mult))
                c.link(nc.vector.tensor_reduce(r_n[:, :], r_c[:, :, 0:n], X_AXIS, ALU.max))
                c.link(nc.vector.tensor_tensor(oh[:, :, 0:n], r_c[:, :, 0:n], bc(r_n[:, :], n), ALU.is_equal))

            def front(item, b, c, n):
                if item == "conv":
                    dve.wait_ge(s["conv_ps"], b + 1)
                    if not (isinstance(b, int) and b == 0):
                        dve.wait_ge(s["comb_sb"], b)
                    c.link(nc.vector.tensor_tensor(
                        h_cur[:, :, :].rearrange("p (r w) c -> p r w c", r=R),
                        pair(0).rearrange("p r (w c) -> p r w c", c=C),
                        conv_b[:, :].unsqueeze(1).unsqueeze(1).to_broadcast((P, R, WT, C)), ALU.add))
                    c.link(nc.vector.tensor_scalar(h_cur[:, :, :], h_cur[:, :, :], 0.0, None, ALU.max))
                    norm(c, n, h_cur, x1, "x1_sb")
                elif item == "attn":
                    dve.wait_ge(s["attn_ps"], b + 1)
                    c.link(nc.vector.tensor_tensor(as_pair(h_cur[:, :, :]), as_pair(h_cur[:, :, :]), pair(0), ALU.add))
                    norm(c, n, h_cur, xr, "xr_sb")
                elif item == "xrt":
                    dve.wait_ge(s["xr_sb"], b + 1)
                    norm(c, n, xr, xf, "xf_sb")
                elif item == "route":
                    dve.wait_ge(s["route_ps"], b + 1)
                    c.link(nc.vector.tensor_copy(r_c[:, :, 0:E0], ps[:, 0, 0:NT * E0].rearrange("p (t e) -> p t e", e=E0)))
                    soft_before(c, "logit_sb", E0)
                    soft_after(c, "exp_sb", b + 1, E0)
                    c.link(nc.vector.tensor_tensor(r_a[:, :, 0:E0], r_p[:, :, 0:E0], oh[:, :, 0:E0], ALU.mult))
                    c.link(nc.vector.tensor_tensor(r_c[:, :, 0:E0], r_p[:, :, 0:E0], r_a[:, :, 0:E0], ALU.subtract))
                    c.link(nc.vector.tensor_reduce(r_n[:, :], r_c[:, :, 0:E0], X_AXIS, ALU.max))
                    c.link(nc.vector.scalar_tensor_tensor(r_n[:, :], r_m[:, :], GATE_EPS, r_n[:, :], ALU.add, ALU.add))
                    c.link(nc.vector.reciprocal(r_g[:, :], r_n[:, :]))
                    c.link(nc.vector.tensor_tensor(r_n[:, :], r_m[:, :], r_g[:, :], ALU.mult))
                    c.link(nc.vector.tensor_tensor(comb_next[:, :, :], oh[:, :, 0:E0], bc(r_n[:, :], E0), ALU.mult))
                elif item == "handover":
                    need(dve, s["h2_sb"], b)
                    c.link(nc.vector.tensor_copy(h_acc[:, :, :], h_cur[:, :, :]))
                    nc.vector.tensor_copy(comb[:, :, :], comb_next[:, :, :]).then_inc(s["comb_sb"], 1)

            def ffn(item, b, c):
                if item[0] == "down" and item[2] == NT - 1:
                    e = item[1]
                    dve.wait_ge(s["down_ps"], E0 * b + e + 1)
                    if e == 0:
                        dve.wait_ge(s["comb_sb"], b + 1)
                    else:
                        dve.wait_ge(s["ffn_acc"], E0 * b + e)
                    for t in range(NT):
                        last = nc.vector.scalar_tensor_tensor(h_acc[:, t, :], pair_tile(3, t), comb[:, t, e:e + 1], h_acc[:, t, :],
                                                              ALU.mult, ALU.add)
                    last.then_inc(s["ffn_acc"], 1)
                elif item[0] == "end":
                    dve.wait_ge(s["ffn_acc"], E0 * (b + 1))
                    need(dve, s["h_stored"], b)
                    nc.vector.tensor_copy(h_two[:, :, :], h_acc[:, :, :]).then_inc(s["h2_sb"], 1)

            def back(item, b, c, n, alone):
                if item == "x3n":
                    dve.wait_ge(s["h2_sb"], b + 1)
                    norm(c, n, h_two, x3, "x3_sb")
                elif item == "v":
                    dve.wait_ge(s["v_ps"], b + 1)
                    settle(dve, s["dve_passed"])
                    nc.vector.tensor_copy(
                        v_all[:, bass.ds(b, 1), :, 0:HD].rearrange("p a (r k) d -> p (a r) k d", r=R),
                        pair(0).rearrange("p r (k d) -> p r k d", d=HD)).then_inc(s["v_sb"], 1)
                elif item != "x3t":
                    k = int(item[2])
                    if alone and k:
                        dve.wait_ge(s["qk_split"], 4 * b + k)
                    dve.wait_ge(s["part1_sb"], 4 * b + k + 1)
                    c.link(nc.vector.scalar_tensor_tensor(as_pair(rest[:, :]), pair(qk_pair(k, alone)), 2.0 * HD ** -0.5 if k % 2 == 0 else 1.0,
                                                          as_pair(parts[:, k, 0, :]), ALU.mult, ALU.subtract))
                    c.link(nc.vector.tensor_copy(parts[:, k, 1, :], rest[:, :]))
                    nc.vector.tensor_tensor(parts[:, k, 2, :], rest[:, :], parts[:, k, 1, :], ALU.subtract).then_inc(s["qk_split"], 1)

            STEADY = 37
            BACK_N = 10
            FRONT_N = STEADY - BACK_N

            def run(i, items):
                if isinstance(i, int):
                    base = FRONT_N * min(i, B) + BACK_N * max(0, i - 2)
                else:
                    base = STEADY * i - 2 * BACK_N
                c = Chain(dve, s["dve_step"], base)
                n = 0
                for kind, item in items:
                    if kind == "front":
                        front(item, i, c, norm_base(i) + n)
                        n += item in ("conv", "attn", "xrt")
                    elif kind == "ffn":
                        ffn(item, i - 1, c)
                    else:
                        back(item, i - 2, c, norm_base(i) + n, is_alone(i))
                        n += item == "x3n"
                fronts = any(k == "front" for k, _ in items)
                backs = any(k == "back" for k, _ in items)
                assert c.n == FRONT_N * fronts + BACK_N * backs, (c.n, fronts, backs)

            both = first_part(run)
            with dve.Fori(2, B) as i:
                run(i, both)
            run(B, plan(False, True, True))
            run(B + 1, plan(False, False, True))
            first_steps = FRONT_N * B + BACK_N * B
            dve.wait_ge(s["v_sb"], B)
            for n in range(4):
                dve.wait_ge(parts_stored[n], 16 * H * B)
            for i in range(SLOTS):
                last = nc.vector.memset(k_st[i][SHIFT0:STACK, :], 1.0)
            last.then_inc(s["p1_done"], 1)

            def row_max(j, slot, t):
                n = NT * j + t
                dve.wait_ge(s["row_scored"], n + 1)
                if t == 0:
                    need(dve, s["stat_saved"], j - SLOTS + 1)
                nc.vector.tensor_reduce(stat[slot][:, 0, t:t + 1], ps[:, 2 * (t % 2):2 * (t % 2) + 2, 0:W],
                                        XY_AXES, ALU.max, negate=True).then_inc(s["neg_max"], 1)

            def row_min(j, slot, t):
                n = NT * j + t
                dve.wait_ge(s["row_exp"], n + 1)
                nc.vector.tensor_reduce(stat[slot][:, 2, t:t + 1], f_ring[(NT * slot + t) % 4][:, :, :],
                                        XY_AXES, ALU.min).then_inc(s["min_done"], 1)

            def turn_max(j, slot):
                dve.wait_ge(s["max_parts"], j + 1)
                nc.vector.transpose(mp_t[slot][:, :], mp[slot % 2][:, :]).then_inc(s["max_turned"], 1)

            def steps(g, first):
                for slot in range(SLOTS):
                    j = g * SLOTS + slot
                    for t in range(NT):
                        row_max(j, slot, t)
                        if t == 3 and not (first and slot == 0):
                            turn_max(j - 1, (slot - 1) % SLOTS)
                        n = NT * slot + t - 2
                        if first and n < 0:
                            continue
                        row_min(g * SLOTS + n // NT, (n // NT) % SLOTS, n % NT)

            steps(0, True)
            with dve.Fori(1, BODIES) as g:
                steps(g, False)
            turn_max(STEPS - 1, SLOTS - 1)
            for t in range(NT - 2, NT):
                row_min(STEPS - 1, SLOTS - 1, t)

            def weighted(b):
                return o_all[:, bass.ds(b * H * 2, H * 2), :].rearrange("p k (t v) -> p k t v", v=VD)

            def stats(b, c):
                settle(dve, s["dve_passed"])
                st = stat_all[:, bass.ds(b * H * 2, H * 2), :].rearrange("p k (q t) -> p k q t", t=NT)
                c.mark(nc.vector.tensor_copy(sum_p[:, :, :], weighted(b)[:, :, :, HD]))
                c.mark(nc.vector.tensor_copy(sq_p[:, :, :], st[:, :, 1, :]))
                c.link(nc.vector.tensor_copy(low_p[:, :, :], st[:, :, 2, :]))
                c.link(nc.vector.tensor_scalar(sum_p[:, :, :], sum_p[:, :, :], 0.5, None, ALU.max))
                c.link(nc.vector.reciprocal(inv_s[:, :, :], sum_p[:, :, :]))
                c.mark(nc.vector.tensor_tensor(sum_p[:, :, :], sum_p[:, :, :], inv_s[:, :, :], ALU.mult))
                c.link(nc.vector.tensor_tensor(sq_p[:, :, :], sq_p[:, :, :], inv_s[:, :, :], ALU.mult))
                var = pw_in[:, :].rearrange("p (k t) -> p k t", t=NT)
                c.mark(nc.vector.tensor_tensor(var, sum_p[:, :, :], sum_p[:, :, :], ALU.mult))
                c.link(nc.vector.tensor_tensor(sq_p[:, :, :], sq_p[:, :, :], inv_s[:, :, :], ALU.mult))
                c.link(nc.vector.scalar_tensor_tensor(var, var, -1.0 / L, sq_p[:, :, :], ALU.mult, ALU.add))
                nc.vector.tensor_scalar(var, var, 0.0, 1.0 / (L - 1), ALU.max, ALU.mult).then_inc(s["pow_in"], 1)

            def chain(item, b, parity, c):
                if item == "feat":
                    dve.wait_ge(s["pow_out"], b + 1)
                    low = low_p[:, :, :]
                    std = pw_out[:, :].rearrange("p (k t) -> p k t", t=NT)
                    c.link(nc.vector.tensor_tensor(low, low, inv_s[:, :, :], ALU.mult))
                    for f, src in enumerate((sum_p[:, :, :], std, inv_s[:, :, :], low)):
                        fv = feat[:, :, :, :, f].rearrange("p w h m -> p w (h m)")
                        c.mark(nc.vector.tensor_tensor(fv, src[:, :, 0:WT].rearrange("p k w -> p w k"),
                                                       src[:, :, WT:NT].rearrange("p k w -> p w k"), ALU.add))
                    c.sync()
                    fm = feat[:, :, :, :, :].rearrange("p w h m f -> p (w h m) f")
                    c.link(nc.vector.tensor_scalar(fm[:, :, 0], fm[:, :, 0], 1.0 / L, None, ALU.mult))
                    nc.vector.tensor_scalar(feat[:, :, :, :, :].rearrange("p w h m f -> p (w h m f)"),
                                            feat[:, :, :, :, :].rearrange("p w h m f -> p (w h m f)"), 0.5, None, ALU.mult
                                            ).then_inc(s["feat_ready"], 1)
                elif item == "fuse":
                    dve.wait_ge(s["g3_sb"], b + 1)
                    c.link(nc.vector.tensor_scalar(beta[:, :, :], alpha[:, :, :], 1.0, None, ALU.add))
                    c.link(nc.vector.reciprocal(alpha[:, :, :], beta[:, :, :]))
                    c.link(nc.vector.tensor_scalar(beta[:, :, :], alpha[:, :, :], -1.0, 1.0, ALU.mult, ALU.add))
                    inv = inv_s[:, :, :].rearrange("p (h m) t -> p m h t", m=2)
                    for m, a in enumerate((alpha, beta)):
                        for r in range(R):
                            c.mark(nc.vector.tensor_tensor(coef[:, m, :, r * WT:(r + 1) * WT], inv[:, m, :, r * WT:(r + 1) * WT],
                                                           a[:, :, :].rearrange("p w h -> p h w"), ALU.mult))
                    c.sync()
                    settle(dve, s["dve_passed"])
                    for m in range(2):
                        c.mark(nc.vector.tensor_tensor(
                            fo[m][:, :, :, :].rearrange("p t h d -> p h t d"),
                            weighted(b).rearrange("p (h m) t v -> p m h t v", m=2)[:, m, :, :, 0:HD],
                            coef[:, m, :, :].unsqueeze(3).to_broadcast((P, H, NT, HD)), ALU.mult))
                    c.sync()
                    nc.vector.tensor_tensor(fo[0][:, :, :, :], fo[0][:, :, :, :], fo[1][:, :, :, :], ALU.add).then_inc(s["fused"], 1)
                elif item == "wo":
                    dve.wait_ge(s["wo_ps"], b + 1)
                    settle(dve, s["dve_passed"])
                    c.link(nc.vector.tensor_tensor(as_pair(h3[:, :, :]),
                                                   h_all[:, bass.ds(b, 1), :].rearrange("p a (r c) -> p (a r) c", r=R),
                                                   pair(1), ALU.add))
                    norm_stats(c, h3)
                elif item == "x4":
                    normalise(NLN0 * B + b, h3, x4, "x4_sb")
                elif item == "route":
                    dve.wait_ge(s["route1_ps"], b + 1)
                    c.link(nc.vector.tensor_tensor(r_c[:, :, :], ps[:, 2, 0:NT * E1].rearrange("p (t e) -> p t e", e=E1),
                                                   sw_b[:, :].unsqueeze(1).to_broadcast((P, NT, E1)), ALU.add))
                    soft_before(c, "logit1_sb", E1)
                elif item == "pick":
                    soft_after(c, "exp1_sb", b + 1, E1)
                    nc.vector.tensor_tensor(ohs[:, :, :], oh[:, 0:WT, :], oh[:, WT:NT, :], ALU.add).then_inc(s["onehot"], 1)
                elif item == "mask":
                    dve.wait_ge(s["rank_ps"], b + 1)
                    rk = ps[:, 3, 0:(WT + 1) * E1].rearrange("p (w e) -> p w e", e=E1)
                    c.link(nc.vector.tensor_tensor(r_a[:, 0:WT, :], rk[:, 0:WT, :],
                                                   carry[:, :].unsqueeze(1).to_broadcast((P, WT, E1)), ALU.add))
                    c.mark(nc.vector.tensor_tensor(carry[:, :], rk[:, WT, :], carry[:, :], ALU.add))
                    c.link(nc.vector.tensor_tensor(r_a[:, WT:NT, :], r_a[:, 0:WT, :], oh[:, 0:WT, :], ALU.add))
                    c.link(nc.vector.tensor_tensor(r_c[:, :, :], r_a[:, :, :], oh[:, :, :], ALU.mult))
                    c.link(nc.vector.tensor_reduce(r_n[:, :], r_c[:, :, :], X_AXIS, ALU.add))
                    c.link(nc.vector.tensor_scalar(r_n[:, :], r_n[:, :], float(CAPACITY), None, ALU.is_lt))
                    c.link(nc.vector.tensor_tensor(r_g[:, :], r_n[:, :], r_m[:, :], ALU.mult))
                    c.mark(nc.vector.tensor_tensor(self_c[:, :], r_m[:, :], r_g[:, :], ALU.subtract))
                    nc.vector.tensor_tensor(mask[parity][:, :, :], oh[:, :, :], bc(r_g[:, :], E1), ALU.mult).then_inc(s["mask_sb"], 1)
                    c.sync()
                    need(dve, s["y_stored"], 16 * WT * (b - 1))
                    for t in range(NT):
                        c.mark(nc.vector.scalar_tensor_tensor(y[parity][:, t, :], x4[:, t, :], self_c[:, t:t + 1], h3[:, t, :],
                                                              ALU.mult, ALU.add))
                    c.sync()
                elif item == "bias":
                    dve.wait_ge(s["bias_ps"], b + 1)
                    c.link(nc.vector.tensor_tensor(as_pair(y[parity][:, :, :]), as_pair(y[parity][:, :, :]), pair(1), ALU.add))

            def experts(k, b, parity):
                before = BATCH_OPS * b + (PIECE_OPS[k - 1] if k else 0)
                n = 0
                if k not in SHARED:
                    for u in range(8):
                        t, q, bank = piece(k)[u % 2]
                        e = u // 2
                        if u < 2:
                            dve.wait_ge(s["ex_ps"], 4 * NT * b + 2 * k + u + 1)
                        if u > 1:
                            dve.wait_ge(s["ex_added"], before + u - 1)
                        elif k:
                            dve.wait_ge(s["ex_added"], before)
                        nc.vector.scalar_tensor_tensor(y[parity][:, t, :], ps[:, bank, e * P:(e + 1) * P],
                                                       mask[parity][:, t, 4 * q + e:4 * q + e + 1], y[parity][:, t, :],
                                                       ALU.mult, ALU.add).then_inc(s["ex_added"], 1)
                    n = 8
                if k in ADD_AT:
                    m = ADD_AT.index(k)
                    t0 = piece(SHARED[m])[0][0]
                    dve.wait_ge(s["side_ready"], len(SHARED) * b + m + 1)
                    dve.wait_ge(s["ex_added"], before + n)
                    sums = y[parity][:, t0:t0 + 2, :].rearrange("p t c -> p (t c)")
                    nc.vector.tensor_tensor(sums, sums, side[m % 2], ALU.add).then_inc(s["ex_added"], 1)

            THIRD_N = 53
            STATS_N = 10

            def run(i, parity, chained, experted):
                c = Chain(dve, s["dve_step"], first_steps + STATS_N + THIRD_N * i)
                for kind, item in third_plan(chained, experted):
                    if kind == "experts":
                        experts(item, i - 1, 1 - parity)
                    elif item != "stats":
                        chain(item, i, parity, c)
                    elif not (isinstance(i, int) and i == B - 1):
                        stats(i + 1, c)
                if chained and not (isinstance(i, int) and i == B - 1):
                    assert c.n == THIRD_N, c.n

            dve.wait_ge(s["stat_saved"], STEPS)
            dve.wait_ge(s["o_copied"], STEPS)
            c = Chain(dve, s["dve_step"], first_steps)
            stats(0, c)
            assert c.n == STATS_N, c.n
            third_part(run, dve.Fori)


_INS = ['x', 'L0_tok_W', 'L0_tok_b', 'L0_attn_W_v', 'L0_attn_W_theta', 'L0_ffn_w_gating', 'L0_ffn_gamma', 'L0_ffn_w1',
        'L0_ffn_w2', 'L1_attn_Wq1', 'L1_attn_Wk1', 'L1_attn_Wq2', 'L1_attn_Wk2', 'L1_attn_Wv', 'L1_attn_Wo', 'L1_attn_gw1',
        'L1_attn_gb1', 'L1_attn_gw2', 'L1_attn_gb2', 'L1_attn_gw3', 'L1_attn_gb3', 'L1_ffn_switch_w', 'L1_ffn_switch_b',
        'L1_ffn_expert_w', 'L1_ffn_expert_b']


def kernel(**inputs):
    import numpy as _np
    import concourse.bacc as _bacc
    from concourse import mybir as _mybir
    from concourse.bass_utils import run_bass_kernel_spmd as _run

    nc = _bacc.Bacc("TRN2", target_bir_lowering=False, num_devices=1)
    arrays, args = {}, []
    for name in _INS:
        a = _np.ascontiguousarray(inputs[name])
        arrays[f"in_{name}"] = a
        args.append(nc.dram_tensor(f"in_{name}", a.shape, _mybir.dt.from_np(a.dtype), kind="ExternalInput").ap())
    args.append(nc.dram_tensor("out_0", (B, L, C), F32, kind="ExternalOutput").ap())
    build(nc, *args)
    r = _run(nc, [arrays], core_ids=[0])
    return r.results[0]["out_0"]
```
